# Optimizing a Trainium2 kernel written in Bass

```python
import numpy as np
import jax
import jax.numpy as jnp

def _softmax(x, axis=-1):
    return jax.nn.softmax(x, axis=axis)

def _gelu(x):
    return jax.nn.gelu(x, approximate=True)

def _silu(x):
    return jax.nn.silu(x)

def _sigmoid(x):
    return jax.nn.sigmoid(x)

def _layernorm(x, axis=-1, eps=1e-05):
    m = jnp.mean(x, axis=axis, keepdims=True)
    v = jnp.var(x, axis=axis, keepdims=True)
    return (x - m) / jnp.sqrt(v + eps)

def _scatter_add(tgt, idx, src, axis=0):
    return tgt.at[idx].add(src)

def _segment_sum(src, seg, n):
    return jax.ops.segment_sum(src, seg, n)
kernel_name = 'mk_seq_postln_d1_jaxref_r8_bd2d6f'

def setup_inputs(seed: int=0):
    np.random.seed(seed)
    _w = jnp.asarray

    def _L0_attn_setup():
        import jax, jax.numpy as jnp
        import numpy as np
        import math
        B, S, H, M, NH = (4, 128, 128, 4096, 1)

        def _reference_tuple_inner(hidden_states, Wq, bq, Wk, bk, Wv, bv, Wo, bo, memory_keys, memory_values, memory_age):
            b, s, _ = hidden_states.shape
            q = (hidden_states @ Wq.T + bq).reshape(b, s, NH, -1)
            k = (hidden_states @ Wk.T + bk).reshape(b, s, NH, -1)
            v = (hidden_states @ Wv.T + bv).reshape(b, s, NH, -1)
            scores = jnp.einsum('bshd,hmd->bshm', q, memory_keys) / math.sqrt(H)
            probs = jax.nn.softmax(scores, axis=-1)
            mem_out = jnp.einsum('bshm,hmd->bshd', probs, memory_values)
            age = memory_age + 1.0
            importance = probs.sum(axis=(0, 1))
            _, upd_idx = jax.lax.top_k(age + (1.0 - importance), s)
            h_idx = jnp.arange(NH)[:, None]
            src_k = k[0, -1][:, None, :]
            src_v = v[0, -1][:, None, :]
            new_keys = memory_keys.at[h_idx, upd_idx].set(src_k)
            new_values = memory_values.at[h_idx, upd_idx].set(src_v)
            new_age = age.at[h_idx, upd_idx].set(0.0)
            output = mem_out.reshape(b, s, -1) @ Wo.T + bo
            access_counts = jnp.sum(probs > 0.01, axis=(0, 1))
            max_scores = jnp.max(scores, axis=-1).mean()
            memory_usage = jnp.mean((new_age > 0).astype(jnp.float32))
            return (output, access_counts, max_scores, memory_usage, new_keys, new_values, new_age)
        key = jax.random.key(seed)
        ks = jax.random.split(key, 12)
        init = lambda k, shape: jax.random.normal(k, shape, dtype=jnp.float32) * 0.02
        return {'hidden_states': jax.random.normal(ks[0], (B, S, H), dtype=jnp.float32), 'Wq': init(ks[1], (H, H)), 'bq': jnp.zeros((H,), jnp.float32), 'Wk': init(ks[2], (H, H)), 'bk': jnp.zeros((H,), jnp.float32), 'Wv': init(ks[3], (H, H)), 'bv': jnp.zeros((H,), jnp.float32), 'Wo': init(ks[4], (H, H)), 'bo': jnp.zeros((H,), jnp.float32), 'memory_keys': init(ks[5], (NH, M, H)), 'memory_values': init(ks[6], (NH, M, H)), 'memory_age': jnp.zeros((NH, M), jnp.float32)}
    _L0_attn_in = _L0_attn_setup()

    def _L0_ffn_setup():
        import jax, jax.numpy as jnp
        import numpy as np
        D_IN, D_HID = (128, 512)

        def _ternary(key, shape):
            return jax.random.randint(key, shape, -1, 2).astype(jnp.float32)

        def _tlin(x, w, s):
            return jnp.einsum('bsi,oi->bso', x, w) * s
        key = jax.random.key(seed)
        ks = jax.random.split(key, 12)
        inv = lambda fan: 1.0 / np.sqrt(fan).astype(np.float32)
        return {'x': jax.random.normal(ks[0], (4, 256, D_IN), dtype=jnp.float32), 'w1_w': _ternary(ks[1], (D_HID, D_IN)), 'w1_s': jax.random.uniform(ks[2], (D_HID,), dtype=jnp.float32) * inv(D_IN), 'w2_w': _ternary(ks[3], (D_HID, D_IN)), 'w2_s': jax.random.uniform(ks[4], (D_HID,), dtype=jnp.float32) * inv(D_IN), 'h1_w': _ternary(ks[5], (D_HID, D_HID)), 'h1_s': jax.random.uniform(ks[6], (D_HID,), dtype=jnp.float32) * inv(D_HID), 'h2_w': _ternary(ks[7], (D_HID, D_HID)), 'h2_s': jax.random.uniform(ks[8], (D_HID,), dtype=jnp.float32) * inv(D_HID), 'w3_w': _ternary(ks[9], (D_IN, D_HID)), 'w3_s': jax.random.uniform(ks[10], (D_IN,), dtype=jnp.float32) * inv(D_HID)}
    _L0_ffn_in = _L0_ffn_setup()
    _d = {'L0_attn_hidden_states': _L0_attn_in['hidden_states'], 'L0_attn_Wq': _L0_attn_in['Wq'], 'L0_attn_bq': _L0_attn_in['bq'], 'L0_attn_Wk': _L0_attn_in['Wk'], 'L0_attn_bk': _L0_attn_in['bk'], 'L0_attn_Wv': _L0_attn_in['Wv'], 'L0_attn_bv': _L0_attn_in['bv'], 'L0_attn_Wo': _L0_attn_in['Wo'], 'L0_attn_bo': _L0_attn_in['bo'], 'L0_attn_memory_keys': _L0_attn_in['memory_keys'], 'L0_attn_memory_values': _L0_attn_in['memory_values'], 'L0_attn_memory_age': _L0_attn_in['memory_age'], 'L0_ffn_w1_w': _L0_ffn_in['w1_w'], 'L0_ffn_w1_s': _L0_ffn_in['w1_s'], 'L0_ffn_w2_w': _L0_ffn_in['w2_w'], 'L0_ffn_w2_s': _L0_ffn_in['w2_s'], 'L0_ffn_h1_w': _L0_ffn_in['h1_w'], 'L0_ffn_h1_s': _L0_ffn_in['h1_s'], 'L0_ffn_h2_w': _L0_ffn_in['h2_w'], 'L0_ffn_h2_s': _L0_ffn_in['h2_s'], 'L0_ffn_w3_w': _L0_ffn_in['w3_w'], 'L0_ffn_w3_s': _L0_ffn_in['w3_s']}
    _x0 = _d['L0_attn_hidden_states']
    _d['L0_attn_hidden_states'] = jax.random.normal(jax.random.fold_in(jax.random.key(seed), 1), (32, 256, 128), dtype=_x0.dtype)
    del _x0
    return _d

def reference(L0_attn_hidden_states, L0_attn_Wq, L0_attn_bq, L0_attn_Wk, L0_attn_bk, L0_attn_Wv, L0_attn_bv, L0_attn_Wo, L0_attn_bo, L0_attn_memory_keys, L0_attn_memory_values, L0_attn_memory_age, L0_ffn_w1_w, L0_ffn_w1_s, L0_ffn_w2_w, L0_ffn_w2_s, L0_ffn_h1_w, L0_ffn_h1_s, L0_ffn_h2_w, L0_ffn_h2_s, L0_ffn_w3_w, L0_ffn_w3_s):

    def _L0_attn_ref(hidden_states, Wq, bq, Wk, bk, Wv, bv, Wo, bo, memory_keys, memory_values, memory_age):
        import jax, jax.numpy as jnp
        import numpy as np
        import math
        B, S, H, M, NH = (4, 128, 128, 4096, 1)

        def _reference_tuple_inner(hidden_states, Wq, bq, Wk, bk, Wv, bv, Wo, bo, memory_keys, memory_values, memory_age):
            b, s, _ = hidden_states.shape
            q = (hidden_states @ Wq.T + bq).reshape(b, s, NH, -1)
            k = (hidden_states @ Wk.T + bk).reshape(b, s, NH, -1)
            v = (hidden_states @ Wv.T + bv).reshape(b, s, NH, -1)
            scores = jnp.einsum('bshd,hmd->bshm', q, memory_keys) / math.sqrt(H)
            probs = jax.nn.softmax(scores, axis=-1)
            mem_out = jnp.einsum('bshm,hmd->bshd', probs, memory_values)
            age = memory_age + 1.0
            importance = probs.sum(axis=(0, 1))
            _, upd_idx = jax.lax.top_k(age + (1.0 - importance), s)
            h_idx = jnp.arange(NH)[:, None]
            src_k = k[0, -1][:, None, :]
            src_v = v[0, -1][:, None, :]
            new_keys = memory_keys.at[h_idx, upd_idx].set(src_k)
            new_values = memory_values.at[h_idx, upd_idx].set(src_v)
            new_age = age.at[h_idx, upd_idx].set(0.0)
            output = mem_out.reshape(b, s, -1) @ Wo.T + bo
            access_counts = jnp.sum(probs > 0.01, axis=(0, 1))
            max_scores = jnp.max(scores, axis=-1).mean()
            memory_usage = jnp.mean((new_age > 0).astype(jnp.float32))
            return (output, access_counts, max_scores, memory_usage, new_keys, new_values, new_age)
        return _reference_tuple_inner(hidden_states, Wq, bq, Wk, bk, Wv, bv, Wo, bo, memory_keys, memory_values, memory_age)[0]

    def _L0_ffn_ref(x, w1_w, w1_s, w2_w, w2_s, h1_w, h1_s, h2_w, h2_s, w3_w, w3_s):
        import jax, jax.numpy as jnp
        import numpy as np
        D_IN, D_HID = (128, 512)

        def _ternary(key, shape):
            return jax.random.randint(key, shape, -1, 2).astype(jnp.float32)

        def _tlin(x, w, s):
            return jnp.einsum('bsi,oi->bso', x, w) * s
        h = jax.nn.silu(_tlin(x, w1_w, w1_s)) * _tlin(x, w2_w, w2_s)
        h = jax.nn.gelu(_tlin(h, h1_w, h1_s), approximate=False)
        h = jax.nn.gelu(_tlin(h, h2_w, h2_s), approximate=False)
        return _tlin(h, w3_w, w3_s)
    x = L0_attn_hidden_states
    x = _layernorm(x + _L0_attn_ref(x, L0_attn_Wq, L0_attn_bq, L0_attn_Wk, L0_attn_bk, L0_attn_Wv, L0_attn_bv, L0_attn_Wo, L0_attn_bo, L0_attn_memory_keys, L0_attn_memory_values, L0_attn_memory_age), axis=-1)
    x = _layernorm(x + _L0_ffn_ref(x, L0_ffn_w1_w, L0_ffn_w1_s, L0_ffn_w2_w, L0_ffn_w2_s, L0_ffn_h1_w, L0_ffn_h1_s, L0_ffn_h2_w, L0_ffn_h2_s, L0_ffn_w3_w, L0_ffn_w3_s), axis=-1)
    return x

_drawn_inputs = setup_inputs


def setup_inputs(seed=0):
    import zlib

    import numpy as np

    out = dict(_drawn_inputs(seed))
    spreads = {'L0_attn_bq': (0.0, 2.0),
     'L0_attn_bk': (0.0, 0.1),
     'L0_attn_bv': (0.0, 0.1),
     'L0_attn_bo': (0.0, 0.79),
     'L0_attn_memory_age': (0.0, 0.1)}
    factors = {'L0_attn_Wq': 64.0,
     'L0_attn_Wo': 64.0,
     'L0_attn_memory_keys': 64.0,
     'L0_attn_memory_values': 60.707,
     'L0_ffn_w1_w': 8.0,
     'L0_ffn_w1_s': 8.0,
     'L0_ffn_w2_w': 8.0,
     'L0_ffn_w2_s': 8.0,
     'L0_ffn_h1_w': 8.0,
     'L0_ffn_h1_s': 8.0,
     'L0_ffn_h2_w': 8.0,
     'L0_ffn_h2_s': 8.0,
     'L0_ffn_w3_w': 8.0,
     'L0_ffn_w3_s': 8.0}
    for name, (base, spread) in spreads.items():
        noise = np.random.default_rng([zlib.crc32(name.encode()), seed]).standard_normal(out[name].shape)
        drawn = base * np.exp(spread * noise) if base else spread * noise
        out[name] = jnp.asarray(drawn.astype(out[name].dtype))
    for name, factor in factors.items():
        out[name] = (out[name] * factor).astype(out[name].dtype)
    return out
```

```python
from contextlib import ExitStack

import numpy as np
import concourse.bass as bass
from concourse import mybir

FP32 = mybir.dt.float32
FP32R = mybir.dt.float32r
FP16 = mybir.dt.float16
ALU = mybir.AluOpType
ACT = mybir.ActivationFunctionType
AX = mybir.AxisListType

P = 128
TOKENS = 32 * 256
SLOTS = 4096
HID = 512
SCALE = float(P) ** -0.5
LIFT = 10.0
EPS = 1e-5

PAIRS = TOKENS // (2 * P)
SC = 512
STEPS = 2 * SLOTS // SC
PIECE = 1024
PIECES = SLOTS // PIECE
T_LAG = 4
PV_LAG = 6

BT = 512
BLOCKS = TOKENS // BT
HC = HID // P


def at_least(eng, sem, value):
    if isinstance(value, int) and value <= 0:
        return
    eng.wait_ge(sem, value)


def valid(index, end):
    return not isinstance(index, int) or 0 <= index < end


def attention(nc, xT, wqT, bq, kT, v, q_dram, o_dram, den):
    ctx = ExitStack()
    with ctx:
        def sb(name, shape, dt):
            return ctx.enter_context(nc.sbuf_tensor(name, shape, dt))

        def sem(name):
            return ctx.enter_context(nc.semaphore(name))

        k_hi = sb("k_hi", [P, SLOTS], FP32R)
        k_lo = sb("k_lo", [P, SLOTS], FP32R)
        v_hi = sb("v_hi", [P, SLOTS // P, P], FP32R)
        v_lo = sb("v_lo", [P, SLOTS // P, P], FP32R)
        s_buf = sb("s_buf", [P, 2, SLOTS], FP32)
        p16 = sb("p16", [P, 2, 2, 2, SLOTS], FP16)
        pT = sb("pT", [P, 4, 2, 4 * P], FP32R)
        q_buf = sb("q_buf", [P, 2, 2, 2 * P], FP32R)
        o_tmp = sb("o_tmp", [P, 2 * P], FP32)
        o_sum = sb("o_sum", [P, 2, 2 * P], FP32)
        ident = sb("ident", [P, P], FP16)
        wq = sb("wq", [P, P], FP32)
        bq_col = sb("bq_col", [P, 1], FP32)
        part_max = sb("part_max", [P, 2, PIECES], FP32)
        row_max = sb("row_max", [P, 2], FP32)
        bias = sb("bias", [P, 2], FP32)
        x_in = sb("x_in", [P, 2, BT], FP32)
        q_f = sb("q_f", [P, 2, BT], FP32)
        q_hl = sb("q_hl", [P, 2, 2, 2, 2 * P], FP32R)

        s_ps = ctx.enter_context(nc.psum_tensor("s_ps", [P, 2, PIECE], FP32))
        t_ps = ctx.enter_context(nc.psum_tensor("t_ps", [P, 2, 2, 4 * P], FP16))
        o_ps = ctx.enter_context(nc.psum_tensor("o_ps", [P, 2, 4 * P], FP32))

        k_loaded, v_loaded, wq_loaded, bq_loaded = map(sem, ("k_loaded", "v_loaded", "wq_loaded", "bq_loaded"))
        x_loaded = [sem("x_loaded0"), sem("x_loaded1")]
        q_stored = [sem("q_stored0"), sem("q_stored1")]
        q_projected, q_moved, q_high, q_split = map(sem, ("q_projected", "q_moved", "q_high", "q_split"))
        ident_ready, k_high, k_split, v_split = map(sem, ("ident_ready", "k_high", "k_split", "v_split"))
        q_loaded = [sem("q_loaded0"), sem("q_loaded1")]
        scored, max_done, bias_ready, exped, highed, split = map(
            sem, ("scored", "max_done", "bias_ready", "exped", "highed", "split"))
        scores_moved, row_maxed = sem("scores_moved"), sem("row_maxed")
        transposed, pT_ready, pv_done = map(sem, ("transposed", "pT_ready", "pv_done"))
        o_half, o_ready = sem("o_half"), sem("o_ready")
        o_stored = [sem("o_stored0"), sem("o_stored1")]

        k_raw, v_raw = s_buf[:, 0, :], s_buf[:, 1, :]
        v_hi_flat = v_hi[:, :, :].rearrange("p c d -> p (c d)")
        v_lo_flat = v_lo[:, :, :].rearrange("p c d -> p (c d)")

        def frames(eng, frame, last):
            frame(0, 0, 0)
            frame(1, 0, 1)
            with eng.Fori(1, PAIRS // 2) as half:
                frame(half * 2, half, 0)
                frame(half * 2 + 1, half, 1)
            for f in range(PAIRS, last):
                frame(f, f // 2, f % 2)

        def q_blocks(eng, block):
            with eng.Fori(0, BLOCKS // 2) as half:
                block(half * 2, half, 0)
                block(half * 2 + 1, half, 1)

        block_ctx = ctx.enter_context(nc.Block())

        @block_ctx.sync
        def _(sp):
            sp.dma_start(wq[:, :], wqT).then_inc(wq_loaded, 16)
            sp.dma_start(bq_col[:, :], bq).then_inc(bq_loaded, 16)
            for b in range(2):
                sp.dma_start(x_in[:, b, :], xT[:, b * BT:(b + 1) * BT]).then_inc(x_loaded[b], 16)
            sp.dma_start(k_raw, kT).then_inc(k_loaded, 16)
            sp.dma_start(v_raw, v).then_inc(v_loaded, 16)

            def store_q(b, b2, par):
                sp.wait_ge(q_split, b + 1)
                sp.dma_start(q_dram[:, bass.ds(b * 2, 2), :, :], q_hl[:, par, :, :, :].bitcast(FP32)).then_inc(q_stored[par], 16)

            def load_x_store_q(b, b2, par):
                sp.wait_ge(q_projected, b + 1)
                sp.dma_start(x_in[:, par, :], xT[:, bass.ds(b * BT + 2 * BT, BT)]).then_inc(x_loaded[par], 16)
                store_q(b, b2, par)

            with sp.Fori(0, BLOCKS // 2 - 1) as half:
                load_x_store_q(half * 2, half, 0)
                load_x_store_q(half * 2 + 1, half, 1)
            for b in range(BLOCKS - 2, BLOCKS):
                store_q(b, b // 2, b % 2)
            for par in range(2):
                sp.wait_ge(q_stored[par], 16 * BLOCKS // 2)

            def load_q(pair, par):
                sp.dma_start(q_buf[:, par, :, :].bitcast(FP32), q_dram[:, pair, :, :]).then_inc(q_loaded[par], 16)

            load_q(0, 0)

            def frame(f, f2, par):
                if valid(f + 1, PAIRS):
                    at_least(sp, scored, 8 * f)
                    load_q(f + 1, 1 - par)
                if valid(f - 2, PAIRS):
                    sp.wait_ge(o_ready, f - 1)
                    sp.dma_start(o_dram[:, bass.ds((f - 2) * 2 * P, 2 * P)], o_sum[:, par, :]).then_inc(o_stored[par], 16)

            frame(0, 0, 0)
            frame(1, 0, 1)
            with sp.Fori(1, PAIRS // 2 - 1) as half:
                frame(half * 2, half, 0)
                frame(half * 2 + 1, half, 1)
            for f in range(PAIRS - 2, PAIRS + 2):
                frame(f, f // 2, f % 2)
            for par in range(2):
                sp.wait_ge(o_stored[par], 16 * PAIRS // 2)

        @block_ctx.gpsimd
        def _(pool):
            nc.gpsimd.memset(ident[:, :], 0.0).then_inc(ident_ready, 1)
            pool.wait_ge(ident_ready, 1)
            nc.gpsimd.affine_select(out=ident[:, :], in_=ident[:, :], compare_op=ALU.not_equal, fill=1.0, base=0,
                                    pattern=[[-1, P]], channel_multiplier=1).then_inc(ident_ready, 1)
            pool.wait_ge(v_loaded, 16)
            nc.gpsimd.tensor_copy(v_hi_flat, v_raw).then_inc(v_split, 1)
            pool.wait_ge(v_split, 1)
            nc.gpsimd.tensor_tensor(v_lo_flat, v_raw, v_hi_flat.bitcast(FP32), ALU.subtract).then_inc(v_split, 1)

        @block_ctx.scalar
        def _(act):
            act.wait_ge(bq_loaded, 16)

            def q_move(b, b2, par):
                act.wait_ge(q_projected, b + 1)
                if par == 0:
                    act.wait_ge(q_split, b2 * 2)
                nc.scalar.activation(q_f[:, par, :], o_ps[:, par, :], ACT.Identity, bias=bq_col[:, :]).then_inc(q_moved, 1)

            q_move_first = [True]
            for b in range(2):
                act.wait_ge(q_projected, b + 1)
                nc.scalar.activation(q_f[:, b, :], o_ps[:, b, :], ACT.Identity, bias=bq_col[:, :]).then_inc(q_moved, 1)
            act.wait_ge(k_loaded, 16)
            nc.scalar.activation(k_hi[:, :], k_raw, ACT.Copy).then_inc(k_high, 1)
            with act.Fori(1, BLOCKS // 2) as half:
                q_move(half * 2, half, 0)
                q_move(half * 2 + 1, half, 1)

            def exp_half(p, tile, half, par):
                act.wait_ge(bias_ready, 2 * p + tile + 1)
                s = s_buf[:, tile, half * SLOTS // 2:(half + 1) * SLOTS // 2]
                nc.scalar.activation(s, s, ACT.Exp, bias=bias[:, tile:tile + 1], scale=SCALE,
                                     accum_out=den[:, bass.ds(4 * p + 2 * tile + half, 1)]).then_inc(exped, 1)

            def frame(f, f2, par):
                for t in range(STEPS):
                    u = 16 * f + (t - 16 - T_LAG)
                    if valid(u, 16 * PAIRS):
                        act.wait_ge(transposed, u + 1)
                        at_least(act, pv_done, u - 3)
                        nc.scalar.activation(pT[:, t % 4, :, :], t_ps[:, t % 2, :, :], ACT.Copy).then_inc(pT_ready, 1)
                    if t in (0, 2) and valid(f - 1, PAIRS):
                        exp_half(f - 1, 1, t // 2, par)
                    if t in (8, 10) and valid(f, PAIRS):
                        exp_half(f, 0, (t - 8) // 2, par)
                    if t == PV_LAG and valid(f - 2, PAIRS):
                        act.wait_ge(pv_done, 16 * f - 16)
                        at_least(act, o_ready, f - 2)
                        nc.scalar.activation(o_tmp[:, :], o_ps[:, par, 2 * P:], ACT.Copy).then_inc(o_half, 1)

            frames(act, frame, PAIRS + 2)

        @block_ctx.vector
        def _(dve):
            def q_parts(b, b2, par, wait_store):
                dve.wait_ge(q_moved, b + 1)
                if wait_store:
                    dve.wait_ge(q_stored[par], 16 * b2)
                hi = q_hl[:, par, :, 0, :]
                lo = q_hl[:, par, :, 1, :]
                src = q_f[:, par, :].rearrange("p (a t) -> p a t", a=2)
                nc.vector.tensor_copy(hi, src).then_inc(q_high, 1)
                dve.wait_ge(q_high, b + 1)
                nc.vector.tensor_tensor(lo, src, hi.bitcast(FP32), ALU.subtract).then_inc(q_split, 1)

            for b in range(2):
                q_parts(b, 0, b, False)
            with dve.Fori(1, BLOCKS // 2) as half:
                q_parts(half * 2, half, 0, True)
                q_parts(half * 2 + 1, half, 1, True)
            dve.wait_ge(k_high, 1)
            nc.vector.tensor_tensor(k_lo[:, :], k_raw, k_hi[:, :].bitcast(FP32), ALU.subtract).then_inc(k_split, 1)
            dve.wait_ge(k_split, 1)

            def p_high(p, tile, k, par):
                dve.wait_ge(exped, 4 * p + 2 * tile + k // 2 + 1)
                if tile == 0 and k == 0:
                    at_least(dve, transposed, 16 * p - 16)
                nc.vector.tensor_copy(p16[:, par, tile, 0, k * PIECE:(k + 1) * PIECE],
                                      s_buf[:, tile, k * PIECE:(k + 1) * PIECE]).then_inc(highed, 1)

            def p_low(p, tile, k, par):
                dve.wait_ge(highed, 8 * p + 4 * tile + k + 1)
                nc.vector.tensor_tensor(p16[:, par, tile, 1, k * PIECE:(k + 1) * PIECE],
                                        s_buf[:, tile, k * PIECE:(k + 1) * PIECE],
                                        p16[:, par, tile, 0, k * PIECE:(k + 1) * PIECE], ALU.subtract).then_inc(split, 1)

            def frame(f, f2, par):
                for j in range(2 * PIECES):
                    tile, k = divmod(j, PIECES)
                    before = (f - 1, 1, k, 1 - par) if tile == 0 else (f, 0, k, par)
                    if valid(before[0], PAIRS):
                        p_high(*before)
                    if valid(f, PAIRS):
                        dve.wait_ge(scored, 8 * f + j + 1)
                        if k == 0:
                            at_least(dve, split, 8 * f - 4 + 4 * tile)
                            if f is 0 and tile == 1:
                                dve.wait_ge(v_split, 2)
                        nc.vector.tensor_scalar(s_buf[:, tile, k * PIECE:(k + 1) * PIECE], s_ps[:, j % 2, :], 1.0, None,
                                                ALU.mult, ALU.max, accum_out=part_max[:, tile, k:k + 1]).then_inc(scores_moved, 1)
                        if k == PIECES - 1:
                            dve.wait_ge(scores_moved, 8 * f + j + 1)
                            nc.vector.reduce_max(row_max[:, tile:tile + 1], part_max[:, tile, :], AX.X).then_inc(row_maxed, 1)
                            dve.wait_ge(row_maxed, 2 * f + tile + 1)
                            nc.vector.tensor_scalar(bias[:, tile:tile + 1], row_max[:, tile:tile + 1], -SCALE, LIFT,
                                                    ALU.mult, ALU.add).then_inc(bias_ready, 1)
                    if valid(before[0], PAIRS):
                        p_low(*before)
                    if j == 4 and valid(f - 2, PAIRS):
                        dve.wait_ge(o_half, f - 1)
                        at_least(dve, o_stored[par], 16 * (f2 - 1))
                        nc.vector.tensor_tensor(o_sum[:, par, :], o_ps[:, par, 0:2 * P], o_tmp[:, :], ALU.add).then_inc(o_ready, 1)

            frames(dve, frame, PAIRS + 2)

        @block_ctx.tensor
        def _(pe):
            pe.wait_ge(wq_loaded, 16)

            def q_project(b, b2, par, wait_moved):
                pe.wait_ge(x_loaded[par], 16 * b2 + 16)
                if wait_moved:
                    pe.wait_ge(q_moved, b - 1)
                nc.tensor.matmul(o_ps[:, par, :], wq[:, :], x_in[:, par, :], start=True, stop=True).then_inc(q_projected, 1)

            for b in range(2):
                q_project(b, 0, b, False)
            with pe.Fori(1, BLOCKS // 2) as half:
                q_project(half * 2, half, 0, True)
                q_project(half * 2 + 1, half, 1, True)
            pe.wait_ge(k_split, 1)
            pe.wait_ge(k_high, 1)
            pe.wait_ge(ident_ready, 2)
            pe.wait_ge(q_moved, BLOCKS)

            def frame(f, f2, par):
                for t in range(STEPS):
                    u = 16 * f + (t - 16 - T_LAG)
                    if valid(u, 16 * PAIRS):
                        p, pp, s = (f - 1, 1 - par, t - T_LAG) if t >= T_LAG else (f - 2, par, t + 16 - T_LAG)
                        if s % 4 == 0:
                            pe.wait_ge(split, 8 * p + 4 + s // 4 + 1)
                        at_least(pe, pT_ready, u - 1)
                        for c in range(2):
                            for part in range(2):
                                for tile in range(2):
                                    at = (2 * s + c) * P
                                    last = nc.tensor.transpose(
                                        t_ps[:, t % 2, c, (2 * part + tile) * P:(2 * part + tile + 1) * P],
                                        p16[:, pp, tile, part, at:at + P], ident[:, :])
                        last.then_inc(transposed, 1)
                    if valid(f, PAIRS):
                        tile, c = divmod(t, STEPS // 2)
                        if t == 0:
                            pe.wait_ge(q_loaded[par], 16 * f2 + 16)
                        if t % 2 == 0:
                            at_least(pe, scores_moved, 8 * f + t // 2 - 1)
                        out = s_ps[:, (t // 2) % 2, (t % 2) * SC:(t % 2 + 1) * SC]
                        q_h = q_buf[:, par, 0, tile * P:(tile + 1) * P]
                        q_l = q_buf[:, par, 1, tile * P:(tile + 1) * P]
                        k_h, k_l = k_hi[:, c * SC:(c + 1) * SC], k_lo[:, c * SC:(c + 1) * SC]
                        nc.tensor.matmul(out, q_h, k_h, start=True, stop=False)
                        nc.tensor.matmul(out, q_h, k_l, start=False, stop=False)
                        last = nc.tensor.matmul(out, q_l, k_h, start=False, stop=True)
                        if t % 2 == 1:
                            last.then_inc(scored, 1)
                    w = 16 * f + (t - 16 - PV_LAG)
                    if valid(w, 16 * PAIRS):
                        p, pp, s = (f - 1, 1 - par, t - PV_LAG) if t >= PV_LAG else (f - 2, par, t + 16 - PV_LAG)
                        pe.wait_ge(pT_ready, w + 1)
                        if s == 0:
                            at_least(pe, o_ready, p - 1)
                            if f is 1:
                                pe.wait_ge(v_split, 2)
                        for c in range(2):
                            first, final = s == 0 and c == 0, s == STEPS - 1 and c == 1
                            nc.tensor.matmul(o_ps[:, pp, :], v_hi[:, 2 * s + c, :], pT[:, (t - PV_LAG) % 4, c, :],
                                             start=first, stop=False, skip_group_check=True)
                            last = nc.tensor.matmul(o_ps[:, pp, 0:2 * P], v_lo[:, 2 * s + c, :],
                                                    pT[:, (t - PV_LAG) % 4, c, 0:2 * P],
                                                    start=False, stop=final, skip_group_check=True)
                        last.then_inc(pv_done, 1)

            frames(pe, frame, PAIRS + 2)


def ffn(nc, x_rows, woT, bo, w_in, w_mid, w_out, s_in, s_mid, s_out, o_dram, den, out_rows):
    ctx = ExitStack()
    with ctx:
        def sb(name, shape, dt):
            return ctx.enter_context(nc.sbuf_tensor(name, shape, dt))

        def sem(name):
            return ctx.enter_context(nc.semaphore(name))

        OFF = {}
        at = 0
        for name, n in (("wo", P), ("w1", HID), ("w2", HID), ("h1", HC * HID), ("h2", HC * HID), ("w3", HC * P)):
            OFF[name] = at
            at += n
        WCOLS = at
        w_raw = sb("w_raw", [P, WCOLS], FP32)
        w_hi = sb("w_hi", [P, WCOLS], FP32R)
        w_lo = sb("w_lo", [P, WCOLS], FP32R)
        scales = sb("scales", [P, 4 * HC + 1], FP32)
        bo_all = sb("bo_all", [P, P], FP32)
        den_sum = sb("den_sum", [P, TOKENS // P], FP32)
        rden = sb("rden", [P, TOKENS // P], FP32)
        ident = sb("ident2", [P, P], FP32)
        minus_half = sb("minus_half", [P, 4], FP32)
        eps = sb("eps", [P, 4], FP32)
        spare = sb("spare", [P, 2], FP32)
        o_in = sb("o_in", [P, 2, BT], FP32)
        x_in = sb("x_in2", [P, 2, 4, P], FP32)
        xb = sb("xb", [P, 4, P], FP32)
        o_hi = sb("o_hi", [P, BT], FP32R)
        o_lo = sb("o_lo", [P, BT], FP32R)
        z1 = sb("z1", [P, 4, P], FP32)
        x1 = sb("x1", [P, 4, P], FP32)
        stats = sb("stats", [P, 2, 4, 6], FP32)
        moments = sb("moments", [P, 2, 4, 2], FP32)
        rstd = sb("rstd", [P, 2, 4], FP32)
        var_eps = sb("var_eps", [P, 2, 4], FP32)
        x1T = sb("x1T", [P, TOKENS], FP32)
        x1_hi = sb("x1_hi", [P, BT], FP32R)
        x1_lo = sb("x1_lo", [P, BT], FP32R)
        gate = sb("gate", [P, 2, BT], FP32)
        prod = sb("prod", [P, 2, BT], FP32)
        gelu = sb("gelu", [P, 2, 2, BT], FP32)
        h_hi = sb("h_hi", [P, 3, HC, BT], FP32R)
        h_lo = sb("h_lo", [P, 3, HC, BT], FP32R)
        z2T = sb("z2T", [P, BT], FP32)
        y_out = sb("y_out", [P, 2, 4, P], FP32)

        ring = ctx.enter_context(nc.psum_tensor("ring", [P, 4, BT], FP32))
        y3_ps = ctx.enter_context(nc.psum_tensor("y3_ps", [P, BT], FP32))
        y_ps = ctx.enter_context(nc.psum_tensor("y_ps", [P, 4, P], FP32))
        x1_ps = ctx.enter_context(nc.psum_tensor("x1_ps", [P, BT], FP32))
        z2_ps = ctx.enter_context(nc.psum_tensor("z2_ps", [P, 4, P], FP32))

        w_loaded, small_loaded = sem("w_loaded"), sem("small_loaded")
        w_high, w_split, rden_ready, const_ready = map(sem, ("w_high", "w_split", "rden_ready", "const_ready"))
        o_loaded = [sem("oo_loaded0"), sem("oo_loaded1")]
        x_loaded = [sem("xx_loaded0"), sem("xx_loaded1")]
        o_high, o_split, xb_ready, y_done = map(sem, ("o_high", "o_split", "xb_ready", "y_done"))
        z1_ready, stats1_ready, moments1_ready, var1_ready, rstd1_ready, x1_ready = map(
            sem, ("z1_ready", "stats1_ready", "moments1_ready", "var1_ready", "rstd1_ready", "x1_ready"))
        x1_transposed, x1T_ready, x1_high, x1_split = map(sem, ("x1_transposed", "x1T_ready", "x1_high", "x1_split"))
        in_done, mid1_done, mid2_done = map(sem, ("in_done", "mid1_done", "mid2_done"))
        gated, prod_ready, prod_high, in_split = map(sem, ("gated", "prod_ready", "prod_high", "in_split"))
        gelu_f = [sem("gelu_f1"), sem("gelu_f2")]
        gelu_h = [sem("gelu_h1"), sem("gelu_h2")]
        gelu_split = [sem("gelu_split1"), sem("gelu_split2")]
        y3_done, z2T_ready, z2_transposed = map(sem, ("y3_done", "z2T_ready", "z2_transposed"))
        stats2_ready, moments2_ready, var2_ready, rstd2_ready, y_ready = map(
            sem, ("stats2_ready", "moments2_ready", "var2_ready", "rstd2_ready", "y_ready"))
        waited = sem("waited")
        y_stored = [sem("y_stored0"), sem("y_stored1")]

        def weight(t, name, k, j, width=HID):
            o = OFF[name] + k * width + j * P
            return t[:, o:o + P]

        FIRST, LAST = -2, BLOCKS

        def turns(eng, turn):
            for i in range(FIRST, 2):
                turn(i, i // 2, i % 2)
            n = (BLOCKS - 4) // 2
            with eng.Fori(1, 1 + n) as half:
                turn(half * 2, half, 0)
                turn(half * 2 + 1, half, 1)
            for i in range(2 + 2 * n, LAST + 1):
                turn(i, i // 2, i % 2)

        block_ctx = ctx.enter_context(nc.Block())

        @block_ctx.sync
        def _(sp):
            def load(b, par, b2):
                sp.dma_start(o_in[:, par, :], o_dram[:, bass.ds(b * BT, BT)]).then_inc(o_loaded[par], 16)
                sp.dma_start(x_in[:, par, :, :], x_rows[:, bass.ds(b * 4, 4), :]).then_inc(x_loaded[par], 16)

            sp.dma_start(w_raw[:, OFF["wo"]:OFF["wo"] + P], woT).then_inc(w_loaded, 16)
            sp.dma_start(w_raw[:, OFF["w1"]:OFF["w1"] + HID], w_in[0]).then_inc(w_loaded, 16)
            sp.dma_start(w_raw[:, OFF["w2"]:OFF["w2"] + HID], w_in[1]).then_inc(w_loaded, 16)
            load(0, 0, 0)
            load(1, 1, 0)
            for n, t in enumerate((w_mid[0], w_mid[1], w_out)):
                o = OFF[("h1", "h2", "w3")[n]]
                wide = t.shape[1]
                cols = HC * wide
                sp.dma_start(w_raw[:, o:o + cols].rearrange("p (k n) -> p k n", k=HC),
                             t.rearrange("(k p) n -> p k n", p=P)).then_inc(w_loaded, 16)
            for n, t in enumerate((s_in[0], s_in[1], s_mid[0], s_mid[1])):
                sp.dma_start(scales[:, n * HC:(n + 1) * HC], t).then_inc(small_loaded, 16)
            sp.dma_start(scales[:, 4 * HC:4 * HC + 1], s_out).then_inc(small_loaded, 16)
            sp.dma_start(bo_all[:, :], bo.partition_broadcast(P)).then_inc(small_loaded, 16)

            def turn(i, i2, par):
                if valid(i - 1, BLOCKS):
                    sp.wait_ge(y_ready, 4 * i)
                    sp.dma_start(out_rows[:, bass.ds(4 * (i - 1), 4), :], y_out[:, 1 - par, :, :]).then_inc(y_stored[1 - par], 16)
                if valid(i + 2, BLOCKS) and valid(i + 4, BLOCKS):
                    sp.wait_ge(o_split, i + 3)
                    sp.wait_ge(xb_ready, i + 3)
                    load(i + 4, par, 0)

            for i in range(FIRST, 2):
                turn(i, i // 2, i % 2)
            n = (BLOCKS - 6) // 2
            with sp.Fori(1, 1 + n) as half:
                turn(half * 2, half, 0)
                turn(half * 2 + 1, half, 1)
            for i in range(2 + 2 * n, LAST + 1):
                turn(i, i // 2, i % 2)
            for par in range(2):
                sp.wait_ge(y_stored[par], 16 * BLOCKS // 2)

        @block_ctx.gpsimd
        def _(pool):
            nc.gpsimd.memset(ident[:, :], 0.0).then_inc(const_ready, 1)
            nc.gpsimd.memset(minus_half[:, :], -0.5).then_inc(const_ready, 1)
            nc.gpsimd.memset(eps[:, :], EPS).then_inc(const_ready, 1)
            pool.wait_ge(const_ready, 3)
            nc.gpsimd.affine_select(out=ident[:, :], in_=ident[:, :], compare_op=ALU.not_equal, fill=1.0, base=0,
                                    pattern=[[-1, P]], channel_multiplier=1).then_inc(const_ready, 1)
            pool.wait_ge(small_loaded, 6 * 16)

            def add_bias(b, b2, par):
                pool.wait_ge(x_loaded[par], 16 * b2 + 16)
                at_least(pool, z1_ready, 4 * b)
                nc.gpsimd.tensor_tensor(xb[:, :, :], x_in[:, par, :, :],
                                        bo_all[:, :].unsqueeze(1).broadcast_to([P, 4, P]), ALU.add).then_inc(xb_ready, 1)

            def inverse_deviation(b, which, moments_ready, var_ready, ready):
                pool.wait_ge(moments_ready, 4 * b + 4)
                nc.gpsimd.tensor_tensor(var_eps[:, which, :], moments[:, which, :, 1], eps[:, :], ALU.add).then_inc(var_ready, 1)
                pool.wait_ge(var_ready, b + 1)
                nc.gpsimd.tensor_tensor(rstd[:, which, :], var_eps[:, which, :], minus_half[:, :], ALU.pow).then_inc(ready, 1)

            def turn(i, i2, par):
                if valid(i + 2, BLOCKS):
                    add_bias(i + 2, i2 + 1, par)
                if valid(i - 1, BLOCKS):
                    inverse_deviation(i - 1, 1, moments2_ready, var2_ready, rstd2_ready)
                if valid(i + 2, BLOCKS):
                    inverse_deviation(i + 2, 0, moments1_ready, var1_ready, rstd1_ready)

            turns(pool, turn)

        @block_ctx.scalar
        def _(act):
            act.wait_ge(w_loaded, 6 * 16)
            nc.scalar.activation(w_hi[:, :], w_raw[:, :], ACT.Copy).then_inc(w_high, 1)
            act.wait_ge(small_loaded, 6 * 16)

            def o_high_part(b, b2, par):
                act.wait_ge(o_loaded[par], 16 * b2 + 16)
                at_least(act, y_done, b)
                nc.scalar.activation(o_hi[:, :], o_in[:, par, :], ACT.Copy).then_inc(o_high, 1)

            def gates(b):
                for j in range(HC + 1):
                    if j < HC:
                        act.wait_ge(in_done, 8 * b + 2 * j + 1)
                        at_least(act, prod_ready, 4 * b + j - 1)
                        nc.scalar.activation(gate[:, j % 2, :], ring[:, (2 * j) % 4, :], ACT.Silu,
                                             scale=scales[:, j:j + 1]).then_inc(gated, 1)
                    if j >= 1:
                        act.wait_ge(prod_ready, 4 * b + j)
                        if j == 1:
                            at_least(act, mid1_done, 4 * b)
                        nc.scalar.activation(h_hi[:, 0, j - 1, :], prod[:, (j - 1) % 2, :], ACT.Copy).then_inc(prod_high, 1)

            def gelus(b, layer, done, used_by):
                col = (1 + layer) * HC
                for j in range(HC):
                    act.wait_ge(done, 4 * b + j + 1)
                    at_least(act, gelu_split[layer - 1], 4 * b + j - 1)
                    nc.scalar.activation(gelu[:, layer - 1, j % 2, :], ring[:, j, :], ACT.Gelu,
                                         scale=scales[:, col + j:col + j + 1]).then_inc(gelu_f[layer - 1], 1)
                    if j == 0:
                        at_least(act, *used_by)
                    nc.scalar.activation(h_hi[:, layer, j, :], ring[:, j, :], ACT.Gelu,
                                         scale=scales[:, col + j:col + j + 1]).then_inc(gelu_h[layer - 1], 1)

            def turn(i, i2, par):
                if valid(i + 2, BLOCKS):
                    o_high_part(i + 2, i2 + 1, par)
                if valid(i + 1, BLOCKS):
                    gates(i + 1)
                if valid(i, BLOCKS):
                    gelus(i, 2, mid2_done, (y3_done, i))
                if valid(i + 2, BLOCKS):
                    act.wait_ge(x1_transposed, i + 3)
                    nc.scalar.activation(x1T[:, bass.ds((i + 2) * BT, BT)], x1_ps[:, :], ACT.Copy).then_inc(x1T_ready, 1)
                if valid(i + 1, BLOCKS):
                    gelus(i + 1, 1, mid1_done, (mid2_done, 4 * (i + 1)))

            turns(act, turn)

        @block_ctx.vector
        def _(dve):
            nc.vector.tensor_tensor(den_sum[:, :], den[:, 0::2], den[:, 1::2], ALU.add).then_inc(rden_ready, 1)
            dve.wait_ge(rden_ready, 1)
            nc.vector.reciprocal(rden[:, :], den_sum[:, :]).then_inc(rden_ready, 1)
            dve.wait_ge(w_high, 1)
            nc.vector.tensor_tensor(w_lo[:, :], w_raw[:, :], w_hi[:, :].bitcast(FP32), ALU.subtract).then_inc(w_split, 1)
            dve.wait_ge(rden_ready, 2)

            def o_low_part(b, b2, par):
                dve.wait_ge(o_high, b + 1)
                nc.vector.tensor_tensor(o_lo[:, :], o_in[:, par, :], o_hi[:, :].bitcast(FP32), ALU.subtract).then_inc(o_split, 1)

            def products(b):
                for j in range(HC + 1):
                    if j < HC:
                        dve.wait_ge(gated, 4 * b + j + 1)
                        dve.wait_ge(in_done, 8 * b + 2 * j + 2)
                        at_least(dve, prod_high, 4 * b + j - 1)
                        at_least(dve, in_split, 4 * b + j - 1)
                        nc.vector.scalar_tensor_tensor(out=prod[:, j % 2, :], in0=ring[:, (2 * j + 1) % 4, :],
                                                       scalar=scales[:, HC + j:HC + j + 1], in1=gate[:, j % 2, :],
                                                       op0=ALU.mult, op1=ALU.mult).then_inc(prod_ready, 1)
                    if j >= 1:
                        dve.wait_ge(prod_high, 4 * b + j)
                        nc.vector.tensor_tensor(h_lo[:, 0, j - 1, :], prod[:, (j - 1) % 2, :],
                                                h_hi[:, 0, j - 1, :].bitcast(FP32), ALU.subtract).then_inc(in_split, 1)

            def gelu_low(b, layer, j):
                dve.wait_ge(gelu_h[layer - 1], 4 * b + j + 1)
                nc.vector.tensor_tensor(h_lo[:, layer, j, :], gelu[:, layer - 1, j % 2, :],
                                        h_hi[:, layer, j, :].bitcast(FP32), ALU.subtract).then_inc(gelu_split[layer - 1], 1)

            def moments_of(b, which, src, stats_ready, moments_ready):
                for s in range(4):
                    nc.vector.bn_stats(stats[:, which, s, :], src[:, s, :]).then_inc(stats_ready, 1)
                dve.wait_ge(stats_ready, 4 * b + 4)
                nc.vector.memset(spare[:, which:which + 1], 0.0).then_inc(waited, 1)
                for s in range(4):
                    nc.vector.bn_aggr(moments[:, which, s, :], stats[:, which, s, :]).then_inc(moments_ready, 1)

            def normalise(b, which, src, dst, rstd_ready, ready):
                dve.wait_ge(rstd_ready, b + 1)
                for s in range(4):
                    nc.vector.tensor_scalar(dst[:, s, :], src[:, s, :], moments[:, which, s, 0:1], rstd[:, which, s:s + 1],
                                            ALU.subtract, ALU.mult).then_inc(ready, 1)

            def turn(i, i2, par):
                if valid(i + 2, BLOCKS):
                    o_low_part(i + 2, i2 + 1, par)
                if valid(i + 1, BLOCKS):
                    products(i + 1)
                if valid(i - 1, BLOCKS):
                    dve.wait_ge(z2_transposed, i)
                    moments_of(i - 1, 1, z2_ps, stats2_ready, moments2_ready)
                if valid(i + 2, BLOCKS):
                    dve.wait_ge(y_done, i + 3)
                    dve.wait_ge(xb_ready, i + 3)
                    at_least(dve, x1_ready, 4 * (i + 2))
                    for s in range(4):
                        nc.vector.scalar_tensor_tensor(out=z1[:, s, :], in0=y_ps[:, s, :],
                                                       scalar=rden[:, bass.ds(4 * (i + 2) + s, 1)], in1=xb[:, s, :],
                                                       op0=ALU.mult, op1=ALU.add).then_inc(z1_ready, 1)
                    dve.wait_ge(z1_ready, 4 * (i + 3))
                    moments_of(i + 2, 0, z1, stats1_ready, moments1_ready)
                if valid(i - 1, BLOCKS):
                    at_least(dve, y_stored[1 - par], 16 * (i2 - 1 + par))
                    normalise(i - 1, 1, z2_ps, y_out[:, 1 - par, :, :], rstd2_ready, y_ready)
                if valid(i, BLOCKS):
                    gelu_low(i, 2, 0)
                if valid(i + 2, BLOCKS):
                    at_least(dve, x1_transposed, i + 2)
                    normalise(i + 2, 0, z1, x1, rstd1_ready, x1_ready)
                if valid(i, BLOCKS):
                    for j in range(1, HC):
                        gelu_low(i, 2, j)
                if valid(i + 1, BLOCKS):
                    gelu_low(i + 1, 1, 0)
                if valid(i + 2, BLOCKS):
                    dve.wait_ge(x1T_ready, i + 3)
                    at_least(dve, in_done, 8 * (i + 2))
                    src = x1T[:, bass.ds((i + 2) * BT, BT)]
                    nc.vector.tensor_copy(x1_hi[:, :], src).then_inc(x1_high, 1)
                    dve.wait_ge(x1_high, i + 3)
                    nc.vector.tensor_tensor(x1_lo[:, :], src, x1_hi[:, :].bitcast(FP32), ALU.subtract).then_inc(x1_split, 1)
                if valid(i + 1, BLOCKS):
                    for j in range(1, HC):
                        gelu_low(i + 1, 1, j)
                if valid(i, BLOCKS):
                    dve.wait_ge(y3_done, i + 1)
                    at_least(dve, z2_transposed, i)
                    nc.vector.scalar_tensor_tensor(out=z2T[:, :], in0=y3_ps[:, :], scalar=scales[:, 4 * HC:4 * HC + 1],
                                                   in1=x1T[:, bass.ds(i * BT, BT)], op0=ALU.mult, op1=ALU.add).then_inc(z2T_ready, 1)

            turns(dve, turn)

        @block_ctx.tensor
        def _(pe):
            pe.wait_ge(w_split, 1)
            pe.wait_ge(const_ready, 4)

            def split_products(out, pairs, sem_done):
                for n, (wh, wl, hh, hl) in enumerate(pairs):
                    nc.tensor.matmul(out, wh, hh, start=n == 0, stop=False)
                    nc.tensor.matmul(out, wh, hl, start=False, stop=False)
                    last = nc.tensor.matmul(out, wl, hh, start=False, stop=n == len(pairs) - 1)
                last.then_inc(sem_done, 1)

            def layer(b, out, name, j, src, sem_done, width=HID):
                split_products(out, [(weight(w_hi, name, k, j, width), weight(w_lo, name, k, j, width),
                                      h_hi[:, src, k, :], h_lo[:, src, k, :]) for k in range(HC)], sem_done)

            def turn(i, i2, par):
                if valid(i + 1, BLOCKS):
                    b = i + 1
                    pe.wait_ge(x1_split, b + 1)
                    for j in range(HC):
                        for n, name in enumerate(("w1", "w2")):
                            bank = (2 * j + n) % 4
                            if j < 2:
                                at_least(pe, gelu_h[0], 4 * i + bank + 1)
                            elif n == 0:
                                pe.wait_ge(gated, 4 * b + j - 1)
                            else:
                                pe.wait_ge(prod_ready, 4 * b + j - 1)
                            split_products(ring[:, bank, :], [(weight(w_hi, name, 0, j), weight(w_lo, name, 0, j),
                                                               x1_hi[:, :], x1_lo[:, :])], in_done)
                if valid(i - 1, BLOCKS):
                    pe.wait_ge(z2T_ready, i)
                    at_least(pe, y_ready, 4 * (i - 1))
                    for s in range(4):
                        last = nc.tensor.transpose(z2_ps[:, s, :], z2T[:, s * P:(s + 1) * P], ident[:, :])
                    last.then_inc(z2_transposed, 1)
                if valid(i + 2, BLOCKS):
                    pe.wait_ge(o_split, i + 3)
                    at_least(pe, z1_ready, 4 * (i + 2))
                    wh, wl = w_hi[:, 0:P], w_lo[:, 0:P]
                    for s in range(4):
                        oh, ol = o_hi[:, s * P:(s + 1) * P], o_lo[:, s * P:(s + 1) * P]
                        nc.tensor.matmul(y_ps[:, s, :], oh, wh, start=True, stop=False)
                        nc.tensor.matmul(y_ps[:, s, :], oh, wl, start=False, stop=False)
                        last = nc.tensor.matmul(y_ps[:, s, :], ol, wh, start=False, stop=True)
                    last.then_inc(y_done, 1)
                if valid(i, BLOCKS):
                    pe.wait_ge(gelu_split[0], 4 * i + 4)
                    for j in range(HC):
                        if valid(i + 1, BLOCKS):
                            pe.wait_ge(prod_ready, 4 * (i + 1) + 3 + j // 2)
                        else:
                            pe.wait_ge(gelu_h[0], 4 * i + j + 1)
                        layer(i, ring[:, j, :], "h2", j, 1, mid2_done)
                if valid(i + 2, BLOCKS):
                    pe.wait_ge(x1_ready, 4 * (i + 3))
                    at_least(pe, x1T_ready, i + 2)
                    for s in range(4):
                        last = nc.tensor.transpose(x1_ps[:, s * P:(s + 1) * P], x1[:, s, :], ident[:, :])
                    last.then_inc(x1_transposed, 1)
                if valid(i + 1, BLOCKS):
                    pe.wait_ge(in_split, 4 * (i + 1) + 4)
                    for j in range(HC):
                        if valid(i, BLOCKS):
                            pe.wait_ge(gelu_h[1], 4 * i + j + 1)
                        else:
                            pe.wait_ge(prod_ready, 4 * (i + 1) + 3 + j // 2)
                        layer(i + 1, ring[:, j, :], "h1", j, 0, mid1_done)
                if valid(i, BLOCKS):
                    pe.wait_ge(gelu_split[1], 4 * i + 4)
                    at_least(pe, z2T_ready, i)
                    layer(i, y3_ps[:, :], "w3", 0, 2, y3_done, P)

            turns(pe, turn)


_OUTS = [((32, 256, P), "float32")]


def program(nc, t, out):
    q_dram = nc.dram_tensor("q_scratch", (P, PAIRS, 2, 2 * P), FP32).ap()
    o_dram = nc.dram_tensor("o_scratch", (P, TOKENS), FP32).ap()
    with nc.sbuf_tensor("den", [P, 2 * TOKENS // P], FP32) as den:
        attention(nc, t["xT"], t["wqT"], t["bq"], t["kT"], t["v"].rearrange("(c p) d -> p c d", p=P), q_dram, o_dram, den)
        rows = "(t p) d -> p t d"
        ffn(nc, t["x"].rearrange(rows, p=P), t["woT"], t["bo"], (t["w1T"], t["w2T"]), (t["h1T"], t["h2T"]), t["w3T"],
            (t["s1"], t["s2"]), (t["s_h1"], t["s_h2"]), t["s3"], o_dram, den, out.rearrange(rows, p=P))


def kernel(**inputs):
    import concourse.bacc as bacc
    from concourse.bass_utils import run_bass_kernel_spmd

    a = {n: np.asarray(v) for n, v in inputs.items()}
    x = a["L0_attn_hidden_states"].reshape(TOKENS, P)
    lay = np.ascontiguousarray
    arrays = {
        "x": lay(x), "xT": lay(x.T), "wqT": lay(a["L0_attn_Wq"].T), "woT": lay(a["L0_attn_Wo"].T),
        "bq": lay(a["L0_attn_bq"].reshape(P, 1)), "bo": lay(a["L0_attn_bo"]),
        "kT": lay(a["L0_attn_memory_keys"][0].T), "v": lay(a["L0_attn_memory_values"][0]),
        "w1T": lay(a["L0_ffn_w1_w"].T), "w2T": lay(a["L0_ffn_w2_w"].T), "h1T": lay(a["L0_ffn_h1_w"].T),
        "h2T": lay(a["L0_ffn_h2_w"].T), "w3T": lay(a["L0_ffn_w3_w"].T),
        "s1": lay(a["L0_ffn_w1_s"].reshape(HC, P).T), "s2": lay(a["L0_ffn_w2_s"].reshape(HC, P).T),
        "s_h1": lay(a["L0_ffn_h1_s"].reshape(HC, P).T), "s_h2": lay(a["L0_ffn_h2_s"].reshape(HC, P).T),
        "s3": lay(a["L0_ffn_w3_s"].reshape(P, 1)),
    }
    nc = bacc.Bacc("TRN2", target_bir_lowering=False, num_devices=1)
    t = {n: nc.dram_tensor(f"in_{n}", v.shape, mybir.dt.from_np(v.dtype), kind="ExternalInput").ap()
         for n, v in arrays.items()}
    out = nc.dram_tensor("out_0", (TOKENS, P), FP32, kind="ExternalOutput").ap()
    program(nc, t, out)
    r = run_bass_kernel_spmd(nc, [{f"in_{n}": v for n, v in arrays.items()}], core_ids=[0])
    return r.results[0]["out_0"].reshape(32, 256, P)
```

```python
from contextlib import ExitStack

import numpy as np
import concourse.bass as bass
from concourse import mybir

FP32 = mybir.dt.float32
FP32R = mybir.dt.float32r
FP16 = mybir.dt.float16
ALU = mybir.AluOpType
ACT = mybir.ActivationFunctionType
AX = mybir.AxisListType

P = 128
TOKENS = 32 * 256
SLOTS = 4096
HID = 512
SCALE = float(P) ** -0.5
LIFT = 10.0
EPS = 1e-5

PAIRS = TOKENS // (2 * P)
SC = 512
STEPS = 2 * SLOTS // SC
PIECE = 1024
PIECES = SLOTS // PIECE
T_LAG = 6
PV_LAG = 9

BT = 512
BLOCKS = TOKENS // BT
HC = HID // P

W_AT, W_COLS = {}, 0
for _name, _cols in (("w1", HID), ("w2", HID), ("h1", HC * HID), ("h2", HC * HID), ("w3", HC * P)):
    W_AT[_name] = W_COLS
    W_COLS += _cols


def at_least(eng, sem, value):
    if isinstance(value, int) and value <= 0:
        return
    eng.wait_ge(sem, value)


def valid(index, end):
    return not isinstance(index, int) or 0 <= index < end


def attention(nc, xT, wqT, bq, kT, v, weights, o_dram, den, keys, w_raw, low_max):
    ctx = ExitStack()
    with ctx:
        def sb(name, shape, dt):
            return ctx.enter_context(nc.sbuf_tensor(name, shape, dt))

        def sem(name):
            return ctx.enter_context(nc.semaphore(name))

        k_hi, k_lo = keys[:, 0:SLOTS], keys[:, SLOTS:2 * SLOTS]
        v_hi = sb("v_hi", [P, SLOTS // P, P], FP32R)
        v_lo = sb("v_lo", [P, SLOTS // P, P], FP32R)
        s_buf = sb("s_buf", [P, 2, SLOTS], FP32)
        p16 = sb("p16", [P, 2, 2, 2, SLOTS], FP16)
        pT = sb("pT", [P, 4, 2, 4 * P], FP32R)
        q_buf = sb("q_buf", [P, 2, 2, 2 * P], FP32R)
        x_in = sb("x_in", [P, 2 * P], FP32)
        o_tmp = sb("o_tmp", [P, 2 * P], FP32)
        o_sum = sb("o_sum", [P, 2 * P], FP32)
        ident = sb("ident", [P, P], FP16)
        wq = sb("wq", [P, P], FP32)
        bq_col = sb("bq_col", [P, 1], FP32)
        part_max = sb("part_max", [P, 2, PIECES], FP32)
        row_max = sb("row_max", [P, 2], FP32)
        bias = sb("bias", [P, 2], FP32)
        low_parts = sb("low_parts", [P, 4], FP32)
        k_raw = p16[:, 0, 1, :, :].rearrange("p a n -> p (a n)").bitcast(FP32)
        v_raw = p16[:, 1, 1, :, :].rearrange("p a n -> p (a n)").bitcast(FP32)

        s_ps = ctx.enter_context(nc.psum_tensor("s_ps", [P, 2, PIECE], FP32))
        t_ps = ctx.enter_context(nc.psum_tensor("t_ps", [P, 2, 2, 4 * P], FP16))
        o_ps = ctx.enter_context(nc.psum_tensor("o_ps", [P, 2, 4 * P], FP32))

        k_loaded = [sem(f"k_loaded{n}") for n in range(PIECES)]
        v_loaded, wq_loaded, bq_loaded, w_loaded = map(sem, ("v_loaded", "wq_loaded", "bq_loaded", "w_loaded"))
        x_loaded, q_projected, q_high, q_split = map(sem, ("x_loaded", "q_projected", "q_high", "q_split"))
        ident_ready, k_high, k_split, v_high, v_split = map(sem, ("ident_ready", "k_high", "k_split", "v_high", "v_split"))
        scored, bias_ready, exped, highed, split = map(sem, ("scored", "bias_ready", "exped", "highed", "split"))
        scores_moved, row_maxed = sem("scores_moved"), sem("row_maxed")
        transposed, pT_ready, pv_done = map(sem, ("transposed", "pT_ready", "pv_done"))
        o_half, o_ready, o_stored = sem("o_half"), sem("o_ready"), sem("o_stored")
        w_high, w_low, w_maxed, low_found = map(sem, ("w_high", "w_low", "w_maxed", "low_found"))

        v_hi_flat = v_hi[:, :, :].rearrange("p c d -> p (c d)")
        v_lo_flat = v_lo[:, :, :].rearrange("p c d -> p (c d)")

        def piece(t, n):
            return t[:, n * PIECE:(n + 1) * PIECE]

        def frames(eng, frame):
            frame(0, 0)
            frame(1, 1)
            with eng.Fori(1, PAIRS // 2 - 1) as half:
                frame(half * 2, 0)
                frame(half * 2 + 1, 1)
            for f in range(PAIRS - 2, PAIRS + 2):
                frame(f, f % 2)

        def unit_bank(par, j):
            return (par + j + (j >= PIECES)) % 2

        block_ctx = ctx.enter_context(nc.Block())

        @block_ctx.sync
        def _(sp):
            def load_x(pair):
                sp.dma_start(x_in[:, :], xT[:, bass.ds(pair * 2 * P, 2 * P)]).then_inc(x_loaded, 16)

            load_x(0)
            sp.dma_start(wq[:, :], wqT).then_inc(wq_loaded, 16)
            for n in range(PIECES):
                sp.dma_start(piece(k_raw, n), piece(kT, n)).then_inc(k_loaded[n], 16)
                if n == 0:
                    sp.dma_start(bq_col[:, :], bq).then_inc(bq_loaded, 16)
            sp.wait_ge(q_projected, 1)
            load_x(1)
            sp.dma_start(v_raw.rearrange("p (c d) -> p c d", d=P), v).then_inc(v_loaded, 16)
            for name, t in weights.items():
                rows = t.shape[0] // P
                cols = rows * t.shape[1]
                sp.dma_start(w_raw[:, W_AT[name]:W_AT[name] + cols].rearrange("p (k n) -> p k n", k=rows),
                             t.rearrange("(k p) n -> p k n", p=P)).then_inc(w_loaded, 16)

            def frame(f, par):
                if valid(f + 2, PAIRS):
                    sp.wait_ge(q_projected, f + 2)
                    load_x(f + 2)
                if valid(f - 2, PAIRS):
                    sp.wait_ge(o_ready, f - 1)
                    sp.dma_start(o_dram[:, bass.ds((f - 2) * 2 * P, 2 * P)], o_sum[:, :]).then_inc(o_stored, 16)

            frames(sp, frame)
            sp.wait_ge(o_stored, 16 * PAIRS)

        @block_ctx.gpsimd
        def _(pool):
            nc.gpsimd.memset(ident[:, :], 0.0).then_inc(ident_ready, 1)
            pool.wait_ge(ident_ready, 1)
            nc.gpsimd.affine_select(out=ident[:, :], in_=ident[:, :], compare_op=ALU.not_equal, fill=1.0, base=0,
                                    pattern=[[-1, P]], channel_multiplier=1).then_inc(ident_ready, 1)
            pool.wait_ge(w_maxed, 4)
            nc.gpsimd.partition_all_reduce(low_max[:, :], low_parts[:, 3:4], P, bass.bass_isa.ReduceOp.max).then_inc(low_found, 1)
            pool.wait_ge(low_found, 1)

        @block_ctx.scalar
        def _(act):
            def q_high_part(p, par):
                act.wait_ge(q_projected, p + 1)
                at_least(act, scored, 8 * p - 8)
                nc.scalar.activation(q_buf[:, par, 0, :], s_ps[:, 1 - par, 0:2 * P], ACT.Identity,
                                     bias=bq_col[:, :]).then_inc(q_high, 1)

            act.wait_ge(bq_loaded, 16)
            q_high_part(0, 0)
            for n in range(PIECES):
                act.wait_ge(k_loaded[n], 16)
                nc.scalar.activation(piece(k_hi, n), piece(k_raw, n), ACT.Copy).then_inc(k_high, 1)

            def exp_piece(p, tile, k):
                act.wait_ge(bias_ready, 2 * p + tile + 1)
                s = piece(s_buf[:, tile, :], k)
                nc.scalar.activation(s, s, ACT.Exp, bias=bias[:, tile:tile + 1], scale=SCALE,
                                     accum_out=den[:, bass.ds((2 * p + tile) * PIECES + k, 1)]).then_inc(exped, 1)

            def frame(f, par):
                for t in range(STEPS):
                    u = 16 * f + (t - 16 - T_LAG)
                    if valid(u, 16 * PAIRS):
                        act.wait_ge(transposed, u + 1)
                        at_least(act, pv_done, u - 3)
                        nc.scalar.activation(pT[:, t % 4, :, :], t_ps[:, t % 2, :, :], ACT.Copy).then_inc(pT_ready, 1)
                    if t == 8 and valid(f + 1, PAIRS):
                        q_high_part(f + 1, 1 - par)
                    if t < PIECES and valid(f - 1, PAIRS):
                        exp_piece(f - 1, 1, t)
                    if 8 <= t < 8 + PIECES and valid(f, PAIRS):
                        exp_piece(f, 0, t - 8)
                    if f is 0 and t == 12:
                        act.wait_ge(v_loaded, 16)
                        nc.scalar.activation(v_hi_flat, v_raw, ACT.Copy).then_inc(v_high, 1)
                    if t == 12 and valid(f - 2, PAIRS):
                        act.wait_ge(pv_done, 16 * f - 16)
                        at_least(act, o_ready, f - 2)
                        nc.scalar.activation(o_tmp[:, :], o_ps[:, par, 2 * P:], ACT.Copy).then_inc(o_half, 1)

            frames(act, frame)

        @block_ctx.vector
        def _(dve):
            def q_low_part(p, par):
                dve.wait_ge(q_high, p + 1)
                nc.vector.scalar_tensor_tensor(out=q_buf[:, par, 1, :], in0=s_ps[:, 1 - par, 0:2 * P],
                                               scalar=bq_col[:, :], in1=q_buf[:, par, 0, :].bitcast(FP32),
                                               op0=ALU.add, op1=ALU.subtract).then_inc(q_split, 1)

            q_low_part(0, 0)
            for n in range(PIECES):
                dve.wait_ge(k_high, n + 1)
                nc.vector.tensor_tensor(piece(k_lo, n), piece(k_raw, n), piece(k_hi, n).bitcast(FP32), ALU.subtract).then_inc(k_split, 1)

            def p_high(p, tile, k, par):
                dve.wait_ge(exped, 8 * p + 4 * tile + k + 1)
                if tile == 0 and k == 0:
                    at_least(dve, transposed, 16 * p - 16)
                nc.vector.tensor_copy(piece(p16[:, par, tile, 0, :], k), piece(s_buf[:, tile, :], k)).then_inc(highed, 1)

            def p_low(p, tile, k, par):
                dve.wait_ge(highed, 8 * p + 4 * tile + k + 1)
                nc.vector.tensor_tensor(piece(p16[:, par, tile, 1, :], k), piece(s_buf[:, tile, :], k),
                                        piece(p16[:, par, tile, 0, :], k), ALU.subtract).then_inc(split, 1)

            def find_low_weights():
                dve.wait_ge(w_loaded, 16 * len(weights))
                dve.wait_ge(scored, 8 * PAIRS)
                nc.vector.tensor_copy(keys[:, 0:W_COLS], w_raw[:, :]).then_inc(w_high, 1)
                dve.wait_ge(w_high, 1)
                room = 2 * SLOTS - W_COLS
                for n, at in enumerate(range(0, W_COLS, room)):
                    cols = min(room, W_COLS - at)
                    left = keys[:, W_COLS:W_COLS + cols]
                    at_least(dve, w_maxed, n)
                    nc.vector.tensor_tensor(left, w_raw[:, at:at + cols], keys[:, at:at + cols].bitcast(FP32),
                                            ALU.subtract).then_inc(w_low, 1)
                    dve.wait_ge(w_low, n + 1)
                    nc.vector.reduce_max(low_parts[:, n:n + 1], left.bitcast(FP32), AX.X, apply_absolute_value=True).then_inc(w_maxed, 1)
                dve.wait_ge(w_maxed, 3)
                nc.vector.reduce_max(low_parts[:, 3:4], low_parts[:, 0:3], AX.X).then_inc(w_maxed, 1)

            def frame(f, par):
                for j in range(2 * PIECES):
                    tile, k = divmod(j, PIECES)
                    if j == 0:
                        before = (f - 1, 0, PIECES - 1, 1 - par)
                    elif j <= PIECES:
                        before = (f - 1, 1, j - 1, 1 - par)
                    else:
                        before = (f, 0, j - PIECES - 1, par)
                    if j == PIECES and valid(f + 1, PAIRS):
                        q_low_part(f + 1, 1 - par)
                    if valid(f, PAIRS):
                        dve.wait_ge(scored, 8 * f + j + 1)
                        at_least(dve, split, 8 * f - 8 + 4 * tile + k + 1)
                        nc.vector.tensor_scalar(piece(s_buf[:, tile, :], k), s_ps[:, unit_bank(par, j), :], 1.0, None,
                                                ALU.mult, ALU.max, accum_out=part_max[:, tile, k:k + 1]).then_inc(scores_moved, 1)
                    if valid(before[0], PAIRS):
                        p_high(*before)
                    if valid(f, PAIRS) and k == PIECES - 1:
                        dve.wait_ge(scores_moved, 8 * f + j + 1)
                        nc.vector.reduce_max(row_max[:, tile:tile + 1], part_max[:, tile, :], AX.X).then_inc(row_maxed, 1)
                        dve.wait_ge(row_maxed, 2 * f + tile + 1)
                        nc.vector.tensor_scalar(bias[:, tile:tile + 1], row_max[:, tile:tile + 1], -SCALE, LIFT,
                                                ALU.mult, ALU.add).then_inc(bias_ready, 1)
                    if valid(before[0], PAIRS):
                        p_low(*before)
                    if f is 0 and j >= PIECES:
                        dve.wait_ge(v_high, 1)
                        nc.vector.tensor_tensor(piece(v_lo_flat, k), piece(v_raw, k), piece(v_hi_flat, k).bitcast(FP32),
                                                ALU.subtract).then_inc(v_split, 1)
                    if j == 7 and valid(f - 2, PAIRS):
                        dve.wait_ge(o_half, f - 1)
                        at_least(dve, o_stored, 16 * (f - 2))
                        nc.vector.tensor_tensor(o_sum[:, :], o_ps[:, par, 0:2 * P], o_tmp[:, :], ALU.add).then_inc(o_ready, 1)
                if f is PAIRS:
                    find_low_weights()

            frames(dve, frame)

        @block_ctx.tensor
        def _(pe):
            def q_project(p, bank):
                pe.wait_ge(x_loaded, 16 * (p + 1))
                nc.tensor.matmul(s_ps[:, bank, 0:2 * P], wq[:, :], x_in[:, :], start=True, stop=True).then_inc(q_projected, 1)

            pe.wait_ge(wq_loaded, 16)
            q_project(0, 1)

            def frame(f, par):
                if f is 0:
                    pe.wait_ge(q_split, 1)
                if f is 1:
                    pe.wait_ge(ident_ready, 2)
                for t in range(STEPS):
                    u = 16 * f + (t - 16 - T_LAG)
                    if valid(u, 16 * PAIRS):
                        p, pp, s = (f - 1, 1 - par, t - T_LAG) if t >= T_LAG else (f - 2, par, t + 16 - T_LAG)
                        if s % 4 == 0:
                            pe.wait_ge(split, 8 * p + 4 + s // 4 + 1)
                        at_least(pe, pT_ready, u - 1)
                        for c in range(2):
                            for part in range(2):
                                for tile in range(2):
                                    at = (2 * s + c) * P
                                    last = nc.tensor.transpose(
                                        t_ps[:, t % 2, c, (2 * part + tile) * P:(2 * part + tile + 1) * P],
                                        p16[:, pp, tile, part, at:at + P], ident[:, :])
                        last.then_inc(transposed, 1)
                    if valid(f, PAIRS):
                        tile, c = divmod(t, STEPS // 2)
                        j = t // 2
                        if t == STEPS // 2 and valid(f + 1, PAIRS):
                            at_least(pe, scores_moved, 8 * f + 3)
                            q_project(f + 1, par)
                        if t % 2 == 0:
                            if j == PIECES + 1 and valid(f + 1, PAIRS):
                                pe.wait_ge(q_split, f + 2)
                            elif j == PIECES + 1:
                                pe.wait_ge(scores_moved, 8 * f + 4)
                            else:
                                at_least(pe, scores_moved, 8 * f + j - 1 + (j == PIECES))
                            if f is 0 and tile == 0:
                                pe.wait_ge(k_split, j + 1)
                        out = s_ps[:, unit_bank(par, j), (t % 2) * SC:(t % 2 + 1) * SC]
                        q_h = q_buf[:, par, 0, tile * P:(tile + 1) * P]
                        q_l = q_buf[:, par, 1, tile * P:(tile + 1) * P]
                        k_h, k_l = k_hi[:, c * SC:(c + 1) * SC], k_lo[:, c * SC:(c + 1) * SC]
                        nc.tensor.matmul(out, q_h, k_h, start=True, stop=False)
                        nc.tensor.matmul(out, q_h, k_l, start=False, stop=False)
                        last = nc.tensor.matmul(out, q_l, k_h, start=False, stop=True)
                        if t % 2 == 1:
                            last.then_inc(scored, 1)
                    w = 16 * f + (t - 16 - PV_LAG)
                    if valid(w, 16 * PAIRS):
                        p, pp, s = (f - 1, 1 - par, t - PV_LAG) if t >= PV_LAG else (f - 2, par, t + 16 - PV_LAG)
                        pe.wait_ge(pT_ready, w + 1)
                        if s == 0:
                            at_least(pe, o_ready, p - 1)
                            if f is 1:
                                pe.wait_ge(v_split, PIECES)
                        for c in range(2):
                            first, final = s == 0 and c == 0, s == STEPS - 1 and c == 1
                            nc.tensor.matmul(o_ps[:, pp, :], v_hi[:, 2 * s + c, :], pT[:, (t - PV_LAG + T_LAG) % 4, c, :],
                                             start=first, stop=False, skip_group_check=True)
                            last = nc.tensor.matmul(o_ps[:, pp, 0:2 * P], v_lo[:, 2 * s + c, :],
                                                    pT[:, (t - PV_LAG + T_LAG) % 4, c, 0:2 * P],
                                                    start=False, stop=final, skip_group_check=True)
                        last.then_inc(pv_done, 1)

            frames(pe, frame)


def ffn(nc, x_rows, woT, bo, scale_cols, o_dram, den, keys, w_raw, low_max, out_rows):
    ctx = ExitStack()
    with ctx:
        def sb(name, shape, dt):
            return ctx.enter_context(nc.sbuf_tensor(name, shape, dt))

        def sem(name):
            return ctx.enter_context(nc.semaphore(name))

        w_hi = keys[:, 0:W_COLS]
        w_lo = sb("w_lo", [P, W_COLS], FP32R)
        wo_raw = sb("wo_raw", [P, P], FP32)
        wo_hi = sb("wo_hi", [P, P], FP32R)
        wo_lo = sb("wo_lo", [P, P], FP32R)
        scales = sb("scales", [P, 4 * HC + 1], FP32)
        bo_all = sb("bo_all", [P, P], FP32)
        den_sum = sb("den_sum", [P, TOKENS // P], FP32)
        rden = sb("rden", [P, TOKENS // P], FP32)
        ident = sb("ident2", [P, P], FP32)
        minus_half = sb("minus_half", [P, 4], FP32)
        eps = sb("eps", [P, 4], FP32)
        spare = sb("spare", [P, 2], FP32)
        o_in = sb("o_in", [P, 2, BT], FP32)
        x_in = sb("x_in2", [P, 2, 4, P], FP32)
        xb = sb("xb", [P, 4, P], FP32)
        o_hi = sb("o_hi", [P, BT], FP32R)
        o_lo = sb("o_lo", [P, BT], FP32R)
        z1 = sb("z1", [P, 4, P], FP32)
        x1 = sb("x1", [P, 4, P], FP32)
        stats = sb("stats", [P, 2, 4, 6], FP32)
        moments = sb("moments", [P, 2, 4, 2], FP32)
        rstd = sb("rstd", [P, 2, 4], FP32)
        var_eps = sb("var_eps", [P, 2, 4], FP32)
        x1T = sb("x1T", [P, TOKENS], FP32)
        x1_hi = sb("x1_hi", [P, BT], FP32R)
        x1_lo = sb("x1_lo", [P, BT], FP32R)
        gate = sb("gate", [P, 2, BT], FP32)
        prod = sb("prod", [P, 2, BT], FP32)
        gelu = sb("gelu", [P, 2, 2, BT], FP32)
        h_hi = sb("h_hi", [P, 3, HC, BT], FP32R)
        h_lo = sb("h_lo", [P, 3, HC, BT], FP32R)
        z2T = sb("z2T", [P, BT], FP32)
        y_out = sb("y_out", [P, 2, 4, P], FP32)

        ring = ctx.enter_context(nc.psum_tensor("ring", [P, 4, BT], FP32))
        y3_ps = ctx.enter_context(nc.psum_tensor("y3_ps", [P, BT], FP32))
        y_ps = ctx.enter_context(nc.psum_tensor("y_ps", [P, 4, P], FP32))
        x1_ps = ctx.enter_context(nc.psum_tensor("x1_ps", [P, BT], FP32))
        z2_ps = ctx.enter_context(nc.psum_tensor("z2_ps", [P, 4, P], FP32))

        wo_loaded, small_loaded = sem("wo_loaded"), sem("small_loaded")
        wo_high, wo_split, w_split, rden_ready, const_ready = map(
            sem, ("wo_high", "wo_split", "w_split", "rden_ready", "const_ready"))
        o_loaded = [sem("oo_loaded0"), sem("oo_loaded1")]
        x_loaded = [sem("xx_loaded0"), sem("xx_loaded1")]
        o_high, o_split, xb_ready, y_done = map(sem, ("o_high", "o_split", "xb_ready", "y_done"))
        z1_ready, stats1_ready, moments1_ready, var1_ready, rstd1_ready, x1_ready = map(
            sem, ("z1_ready", "stats1_ready", "moments1_ready", "var1_ready", "rstd1_ready", "x1_ready"))
        x1_transposed, x1T_ready, x1_high, x1_split = map(sem, ("x1_transposed", "x1T_ready", "x1_high", "x1_split"))
        in_done, mid1_done, mid2_done = map(sem, ("in_done", "mid1_done", "mid2_done"))
        gated, prod_ready, prod_high, in_split = map(sem, ("gated", "prod_ready", "prod_high", "in_split"))
        gelu_f = [sem("gelu_f1"), sem("gelu_f2")]
        gelu_h = [sem("gelu_h1"), sem("gelu_h2")]
        gelu_split = [sem("gelu_split1"), sem("gelu_split2")]
        y3_done, z2T_ready, z2_transposed = map(sem, ("y3_done", "z2T_ready", "z2_transposed"))
        stats2_ready, moments2_ready, var2_ready, rstd2_ready, y_ready = map(
            sem, ("stats2_ready", "moments2_ready", "var2_ready", "rstd2_ready", "y_ready"))
        waited = sem("waited")
        y_stored = [sem("y_stored0"), sem("y_stored1")]

        def weight(t, name, k, j, width=HID):
            o = W_AT[name] + k * width + j * P
            return t[:, o:o + P]

        FIRST, LAST = -2, BLOCKS

        def turns(eng, turn):
            for i in range(FIRST, 2):
                turn(i, i // 2, i % 2)
            n = (BLOCKS - 4) // 2
            with eng.Fori(1, 1 + n) as half:
                turn(half * 2, half, 0)
                turn(half * 2 + 1, half, 1)
            for i in range(2 + 2 * n, LAST + 1):
                turn(i, i // 2, i % 2)

        block_ctx = ctx.enter_context(nc.Block())

        @block_ctx.sync
        def _(sp):
            def load(b, par, b2):
                sp.dma_start(o_in[:, par, :], o_dram[:, bass.ds(b * BT, BT)]).then_inc(o_loaded[par], 16)
                sp.dma_start(x_in[:, par, :, :], x_rows[:, bass.ds(b * 4, 4), :]).then_inc(x_loaded[par], 16)

            sp.dma_start(wo_raw[:, :], woT).then_inc(wo_loaded, 16)
            load(0, 0, 0)
            load(1, 1, 0)
            for n, t in enumerate(scale_cols):
                sp.dma_start(scales[:, n * HC:n * HC + t.shape[1]], t).then_inc(small_loaded, 16)
            sp.dma_start(bo_all[:, :], bo.partition_broadcast(P)).then_inc(small_loaded, 16)

            def turn(i, i2, par):
                if valid(i - 1, BLOCKS):
                    sp.wait_ge(y_ready, 4 * i)
                    sp.dma_start(out_rows[:, bass.ds(4 * (i - 1), 4), :], y_out[:, 1 - par, :, :]).then_inc(y_stored[1 - par], 16)
                if valid(i + 2, BLOCKS) and valid(i + 4, BLOCKS):
                    sp.wait_ge(o_split, i + 3)
                    sp.wait_ge(xb_ready, i + 3)
                    load(i + 4, par, 0)

            for i in range(FIRST, 2):
                turn(i, i // 2, i % 2)
            n = (BLOCKS - 6) // 2
            with sp.Fori(1, 1 + n) as half:
                turn(half * 2, half, 0)
                turn(half * 2 + 1, half, 1)
            for i in range(2 + 2 * n, LAST + 1):
                turn(i, i // 2, i % 2)
            for par in range(2):
                sp.wait_ge(y_stored[par], 16 * BLOCKS // 2)

        @block_ctx.gpsimd
        def _(pool):
            nc.gpsimd.memset(ident[:, :], 0.0).then_inc(const_ready, 1)
            nc.gpsimd.memset(minus_half[:, :], -0.5).then_inc(const_ready, 1)
            nc.gpsimd.memset(eps[:, :], EPS).then_inc(const_ready, 1)
            pool.wait_ge(const_ready, 3)
            nc.gpsimd.affine_select(out=ident[:, :], in_=ident[:, :], compare_op=ALU.not_equal, fill=1.0, base=0,
                                    pattern=[[-1, P]], channel_multiplier=1).then_inc(const_ready, 1)
            pool.wait_ge(small_loaded, 6 * 16)

            def add_bias(b, b2, par):
                pool.wait_ge(x_loaded[par], 16 * b2 + 16)
                at_least(pool, z1_ready, 4 * b)
                nc.gpsimd.tensor_tensor(xb[:, :, :], x_in[:, par, :, :],
                                        bo_all[:, :].unsqueeze(1).broadcast_to([P, 4, P]), ALU.add).then_inc(xb_ready, 1)

            def inverse_deviation(b, which, moments_ready, var_ready, ready):
                pool.wait_ge(moments_ready, 4 * b + 4)
                nc.gpsimd.tensor_tensor(var_eps[:, which, :], moments[:, which, :, 1], eps[:, :], ALU.add).then_inc(var_ready, 1)
                pool.wait_ge(var_ready, b + 1)
                nc.gpsimd.tensor_tensor(rstd[:, which, :], var_eps[:, which, :], minus_half[:, :], ALU.pow).then_inc(ready, 1)

            def turn(i, i2, par):
                if valid(i + 2, BLOCKS):
                    add_bias(i + 2, i2 + 1, par)
                if valid(i - 1, BLOCKS):
                    inverse_deviation(i - 1, 1, moments2_ready, var2_ready, rstd2_ready)
                if valid(i + 2, BLOCKS):
                    inverse_deviation(i + 2, 0, moments1_ready, var1_ready, rstd1_ready)

            turns(pool, turn)

        @block_ctx.scalar
        def _(act):
            act.wait_ge(wo_loaded, 16)
            nc.scalar.activation(wo_hi[:, :], wo_raw[:, :], ACT.Copy).then_inc(wo_high, 1)
            act.wait_ge(small_loaded, 6 * 16)

            def o_high_part(b, b2, par):
                act.wait_ge(o_loaded[par], 16 * b2 + 16)
                at_least(act, y_done, b)
                nc.scalar.activation(o_hi[:, :], o_in[:, par, :], ACT.Copy).then_inc(o_high, 1)

            def gates(b):
                for j in range(HC + 1):
                    if j < HC:
                        act.wait_ge(in_done, 8 * b + 2 * j + 1)
                        at_least(act, prod_ready, 4 * b + j - 1)
                        nc.scalar.activation(gate[:, j % 2, :], ring[:, (2 * j) % 4, :], ACT.Silu,
                                             scale=scales[:, j:j + 1]).then_inc(gated, 1)
                    if j >= 1:
                        act.wait_ge(prod_ready, 4 * b + j)
                        if j == 1:
                            at_least(act, mid1_done, 4 * b)
                        nc.scalar.activation(h_hi[:, 0, j - 1, :], prod[:, (j - 1) % 2, :], ACT.Copy).then_inc(prod_high, 1)

            def gelus(b, layer, done, used_by):
                col = (1 + layer) * HC
                for j in range(HC):
                    act.wait_ge(done, 4 * b + j + 1)
                    at_least(act, gelu_split[layer - 1], 4 * b + j - 1)
                    nc.scalar.activation(gelu[:, layer - 1, j % 2, :], ring[:, j, :], ACT.Gelu,
                                         scale=scales[:, col + j:col + j + 1]).then_inc(gelu_f[layer - 1], 1)
                    if j == 0:
                        at_least(act, *used_by)
                    nc.scalar.activation(h_hi[:, layer, j, :], ring[:, j, :], ACT.Gelu,
                                         scale=scales[:, col + j:col + j + 1]).then_inc(gelu_h[layer - 1], 1)

            def turn(i, i2, par):
                if valid(i + 2, BLOCKS):
                    o_high_part(i + 2, i2 + 1, par)
                if valid(i + 1, BLOCKS):
                    gates(i + 1)
                if valid(i, BLOCKS):
                    gelus(i, 2, mid2_done, (y3_done, i))
                if valid(i + 2, BLOCKS):
                    act.wait_ge(x1_transposed, i + 3)
                    nc.scalar.activation(x1T[:, bass.ds((i + 2) * BT, BT)], x1_ps[:, :], ACT.Copy).then_inc(x1T_ready, 1)
                if valid(i + 1, BLOCKS):
                    gelus(i + 1, 1, mid1_done, (mid2_done, 4 * (i + 1)))

            turns(act, turn)

        @block_ctx.vector
        def _(dve):
            nc.vector.reduce_sum(den_sum[:, :], den[:, :].rearrange("p (t k) -> p t k", k=PIECES), AX.X).then_inc(rden_ready, 1)
            dve.wait_ge(rden_ready, 1)
            nc.vector.reciprocal(rden[:, :], den_sum[:, :]).then_inc(rden_ready, 1)
            dve.wait_ge(wo_high, 1)
            nc.vector.tensor_tensor(wo_lo[:, :], wo_raw[:, :], wo_hi[:, :].bitcast(FP32), ALU.subtract).then_inc(wo_split, 1)
            low = dve.value_load(low_max[0:1, 0:1].bitcast(mybir.dt.int32))
            with dve.If(low > 0):
                nc.vector.tensor_tensor(w_lo[:, :], w_raw[:, :], w_hi.bitcast(FP32), ALU.subtract).then_inc(w_split, 1)
            with dve.Else():
                nc.vector.memset(spare[:, 0:1], 0.0).then_inc(w_split, 1)
            dve.wait_ge(rden_ready, 2)

            def o_low_part(b, b2, par):
                dve.wait_ge(o_high, b + 1)
                nc.vector.tensor_tensor(o_lo[:, :], o_in[:, par, :], o_hi[:, :].bitcast(FP32), ALU.subtract).then_inc(o_split, 1)

            def products(b):
                for j in range(HC + 1):
                    if j < HC:
                        dve.wait_ge(gated, 4 * b + j + 1)
                        dve.wait_ge(in_done, 8 * b + 2 * j + 2)
                        at_least(dve, prod_high, 4 * b + j - 1)
                        at_least(dve, in_split, 4 * b + j - 1)
                        nc.vector.scalar_tensor_tensor(out=prod[:, j % 2, :], in0=ring[:, (2 * j + 1) % 4, :],
                                                       scalar=scales[:, HC + j:HC + j + 1], in1=gate[:, j % 2, :],
                                                       op0=ALU.mult, op1=ALU.mult).then_inc(prod_ready, 1)
                    if j >= 1:
                        dve.wait_ge(prod_high, 4 * b + j)
                        nc.vector.tensor_tensor(h_lo[:, 0, j - 1, :], prod[:, (j - 1) % 2, :],
                                                h_hi[:, 0, j - 1, :].bitcast(FP32), ALU.subtract).then_inc(in_split, 1)

            def gelu_low(b, layer, j):
                dve.wait_ge(gelu_h[layer - 1], 4 * b + j + 1)
                nc.vector.tensor_tensor(h_lo[:, layer, j, :], gelu[:, layer - 1, j % 2, :],
                                        h_hi[:, layer, j, :].bitcast(FP32), ALU.subtract).then_inc(gelu_split[layer - 1], 1)

            def moments_of(b, which, src, stats_ready, moments_ready):
                for s in range(4):
                    nc.vector.bn_stats(stats[:, which, s, :], src[:, s, :]).then_inc(stats_ready, 1)
                dve.wait_ge(stats_ready, 4 * b + 4)
                nc.vector.memset(spare[:, which:which + 1], 0.0).then_inc(waited, 1)
                for s in range(4):
                    nc.vector.bn_aggr(moments[:, which, s, :], stats[:, which, s, :]).then_inc(moments_ready, 1)

            def normalise(b, which, src, dst, rstd_ready, ready):
                dve.wait_ge(rstd_ready, b + 1)
                for s in range(4):
                    nc.vector.tensor_scalar(dst[:, s, :], src[:, s, :], moments[:, which, s, 0:1], rstd[:, which, s:s + 1],
                                            ALU.subtract, ALU.mult).then_inc(ready, 1)

            def turn(i, i2, par):
                if valid(i + 2, BLOCKS):
                    o_low_part(i + 2, i2 + 1, par)
                if valid(i + 1, BLOCKS):
                    products(i + 1)
                if valid(i - 1, BLOCKS):
                    dve.wait_ge(z2_transposed, i)
                    moments_of(i - 1, 1, z2_ps, stats2_ready, moments2_ready)
                if valid(i + 2, BLOCKS):
                    dve.wait_ge(y_done, i + 3)
                    dve.wait_ge(xb_ready, i + 3)
                    at_least(dve, x1_ready, 4 * (i + 2))
                    for s in range(4):
                        nc.vector.scalar_tensor_tensor(out=z1[:, s, :], in0=y_ps[:, s, :],
                                                       scalar=rden[:, bass.ds(4 * (i + 2) + s, 1)], in1=xb[:, s, :],
                                                       op0=ALU.mult, op1=ALU.add).then_inc(z1_ready, 1)
                    dve.wait_ge(z1_ready, 4 * (i + 3))
                    moments_of(i + 2, 0, z1, stats1_ready, moments1_ready)
                if valid(i - 1, BLOCKS):
                    at_least(dve, y_stored[1 - par], 16 * (i2 - 1 + par))
                    normalise(i - 1, 1, z2_ps, y_out[:, 1 - par, :, :], rstd2_ready, y_ready)
                if valid(i, BLOCKS):
                    gelu_low(i, 2, 0)
                if valid(i + 2, BLOCKS):
                    at_least(dve, x1_transposed, i + 2)
                    normalise(i + 2, 0, z1, x1, rstd1_ready, x1_ready)
                if valid(i, BLOCKS):
                    for j in range(1, HC):
                        gelu_low(i, 2, j)
                if valid(i + 1, BLOCKS):
                    gelu_low(i + 1, 1, 0)
                if valid(i + 2, BLOCKS):
                    dve.wait_ge(x1T_ready, i + 3)
                    at_least(dve, in_done, 8 * (i + 2))
                    src = x1T[:, bass.ds((i + 2) * BT, BT)]
                    nc.vector.tensor_copy(x1_hi[:, :], src).then_inc(x1_high, 1)
                    dve.wait_ge(x1_high, i + 3)
                    nc.vector.tensor_tensor(x1_lo[:, :], src, x1_hi[:, :].bitcast(FP32), ALU.subtract).then_inc(x1_split, 1)
                if valid(i + 1, BLOCKS):
                    for j in range(1, HC):
                        gelu_low(i + 1, 1, j)
                if valid(i, BLOCKS):
                    dve.wait_ge(y3_done, i + 1)
                    at_least(dve, z2_transposed, i)
                    nc.vector.scalar_tensor_tensor(out=z2T[:, :], in0=y3_ps[:, :], scalar=scales[:, 4 * HC:4 * HC + 1],
                                                   in1=x1T[:, bass.ds(i * BT, BT)], op0=ALU.mult, op1=ALU.add).then_inc(z2T_ready, 1)

            turns(dve, turn)

        @block_ctx.tensor
        def _(pe):
            pe.wait_ge(w_split, 1)
            pe.wait_ge(wo_split, 1)
            pe.wait_ge(const_ready, 4)

            def split_products(out, pairs, sem_done, low_weights):
                for n, (wh, wl, hh, hl) in enumerate(pairs):
                    final = n == len(pairs) - 1
                    nc.tensor.matmul(out, wh, hh, start=n == 0, stop=False)
                    last = nc.tensor.matmul(out, wh, hl, start=False, stop=final and not low_weights)
                    if low_weights:
                        last = nc.tensor.matmul(out, wl, hh, start=False, stop=final)
                last.then_inc(sem_done, 1)

            def layer(out, name, j, src, sem_done, low_weights, width=HID):
                split_products(out, [(weight(w_hi, name, k, j, width), weight(w_lo, name, k, j, width),
                                      h_hi[:, src, k, :], h_lo[:, src, k, :]) for k in range(HC)], sem_done, low_weights)

            def turn(i, i2, par, low_weights):
                if valid(i + 1, BLOCKS):
                    b = i + 1
                    pe.wait_ge(x1_split, b + 1)
                    for j in range(HC):
                        for n, name in enumerate(("w1", "w2")):
                            bank = (2 * j + n) % 4
                            if j < 2:
                                at_least(pe, gelu_h[0], 4 * i + bank + 1)
                            elif n == 0:
                                pe.wait_ge(gated, 4 * b + j - 1)
                            else:
                                pe.wait_ge(prod_ready, 4 * b + j - 1)
                            split_products(ring[:, bank, :], [(weight(w_hi, name, 0, j), weight(w_lo, name, 0, j),
                                                               x1_hi[:, :], x1_lo[:, :])], in_done, low_weights)
                if valid(i - 1, BLOCKS):
                    pe.wait_ge(z2T_ready, i)
                    at_least(pe, y_ready, 4 * (i - 1))
                    for s in range(4):
                        last = nc.tensor.transpose(z2_ps[:, s, :], z2T[:, s * P:(s + 1) * P], ident[:, :])
                    last.then_inc(z2_transposed, 1)
                if valid(i + 2, BLOCKS):
                    pe.wait_ge(o_split, i + 3)
                    at_least(pe, z1_ready, 4 * (i + 2))
                    wh, wl = wo_hi[:, :], wo_lo[:, :]
                    for s in range(4):
                        oh, ol = o_hi[:, s * P:(s + 1) * P], o_lo[:, s * P:(s + 1) * P]
                        nc.tensor.matmul(y_ps[:, s, :], oh, wh, start=True, stop=False)
                        nc.tensor.matmul(y_ps[:, s, :], oh, wl, start=False, stop=False)
                        last = nc.tensor.matmul(y_ps[:, s, :], ol, wh, start=False, stop=True)
                    last.then_inc(y_done, 1)
                if valid(i, BLOCKS):
                    pe.wait_ge(gelu_split[0], 4 * i + 4)
                    for j in range(HC):
                        if valid(i + 1, BLOCKS):
                            pe.wait_ge(prod_ready, 4 * (i + 1) + 3 + j // 2)
                        else:
                            pe.wait_ge(gelu_h[0], 4 * i + j + 1)
                        layer(ring[:, j, :], "h2", j, 1, mid2_done, low_weights)
                if valid(i + 2, BLOCKS):
                    pe.wait_ge(x1_ready, 4 * (i + 3))
                    at_least(pe, x1T_ready, i + 2)
                    for s in range(4):
                        last = nc.tensor.transpose(x1_ps[:, s * P:(s + 1) * P], x1[:, s, :], ident[:, :])
                    last.then_inc(x1_transposed, 1)
                if valid(i + 1, BLOCKS):
                    pe.wait_ge(in_split, 4 * (i + 1) + 4)
                    for j in range(HC):
                        if valid(i, BLOCKS):
                            pe.wait_ge(gelu_h[1], 4 * i + j + 1)
                        else:
                            pe.wait_ge(prod_ready, 4 * (i + 1) + 3 + j // 2)
                        layer(ring[:, j, :], "h1", j, 0, mid1_done, low_weights)
                if valid(i, BLOCKS):
                    pe.wait_ge(gelu_split[1], 4 * i + 4)
                    at_least(pe, z2T_ready, i)
                    layer(y3_ps[:, :], "w3", 0, 2, y3_done, low_weights, P)

            low = pe.value_load(low_max[0:1, 0:1].bitcast(mybir.dt.int32))
            with pe.If(low > 0):
                turns(pe, lambda i, i2, par: turn(i, i2, par, True))
            with pe.Else():
                turns(pe, lambda i, i2, par: turn(i, i2, par, False))


def program(nc, t, out):
    o_dram = nc.dram_tensor("o_scratch", (P, TOKENS), FP32).ap()
    with (
        nc.sbuf_tensor("den", [P, PIECES * TOKENS // P], FP32) as den,
        nc.sbuf_tensor("keys", [P, 2 * SLOTS], FP32R) as keys,
        nc.sbuf_tensor("w_raw", [P, W_COLS], FP32) as w_raw,
        nc.sbuf_tensor("low_max", [P, 1], FP32) as low_max,
    ):
        weights = {"w1": t["w1T"], "w2": t["w2T"], "h1": t["h1T"], "h2": t["h2T"], "w3": t["w3T"]}
        attention(nc, t["xT"], t["wqT"], t["bq"], t["kT"], t["v"].rearrange("(c p) d -> p c d", p=P), weights,
                  o_dram, den, keys, w_raw, low_max)
        rows = "(t p) d -> p t d"
        ffn(nc, t["x"].rearrange(rows, p=P), t["woT"], t["bo"], (t["s1"], t["s2"], t["s_h1"], t["s_h2"], t["s3"]),
            o_dram, den, keys, w_raw, low_max, out.rearrange(rows, p=P))


def kernel(**inputs):
    import concourse.bacc as bacc
    from concourse.bass_utils import run_bass_kernel_spmd

    a = {n: np.asarray(v) for n, v in inputs.items()}
    x = a["L0_attn_hidden_states"].reshape(TOKENS, P)
    lay = np.ascontiguousarray
    arrays = {
        "x": lay(x), "xT": lay(x.T), "wqT": lay(a["L0_attn_Wq"].T), "woT": lay(a["L0_attn_Wo"].T),
        "bq": lay(a["L0_attn_bq"].reshape(P, 1)), "bo": lay(a["L0_attn_bo"]),
        "kT": lay(a["L0_attn_memory_keys"][0].T), "v": lay(a["L0_attn_memory_values"][0]),
        "w1T": lay(a["L0_ffn_w1_w"].T), "w2T": lay(a["L0_ffn_w2_w"].T), "h1T": lay(a["L0_ffn_h1_w"].T),
        "h2T": lay(a["L0_ffn_h2_w"].T), "w3T": lay(a["L0_ffn_w3_w"].T),
        "s1": lay(a["L0_ffn_w1_s"].reshape(HC, P).T), "s2": lay(a["L0_ffn_w2_s"].reshape(HC, P).T),
        "s_h1": lay(a["L0_ffn_h1_s"].reshape(HC, P).T), "s_h2": lay(a["L0_ffn_h2_s"].reshape(HC, P).T),
        "s3": lay(a["L0_ffn_w3_s"].reshape(P, 1)),
    }
    nc = bacc.Bacc("TRN2", target_bir_lowering=False, num_devices=1)
    t = {n: nc.dram_tensor(f"in_{n}", v.shape, mybir.dt.from_np(v.dtype), kind="ExternalInput").ap()
         for n, v in arrays.items()}
    out = nc.dram_tensor("out_0", (TOKENS, P), FP32, kind="ExternalOutput").ap()
    program(nc, t, out)
    r = run_bass_kernel_spmd(nc, [{f"in_{n}": v for n, v in arrays.items()}], core_ids=[0])
    return r.results[0]["out_0"].reshape(32, 256, P)
```

```python
from contextlib import ExitStack

import numpy as np
import concourse.bass as bass
from concourse import mybir

FP32 = mybir.dt.float32
FP32R = mybir.dt.float32r
FP16 = mybir.dt.float16
ALU = mybir.AluOpType
ACT = mybir.ActivationFunctionType
AX = mybir.AxisListType

P = 128
TOKENS = 32 * 256
SLOTS = 4096
HID = 512
SCALE = float(P) ** -0.5
LIFT = 10.0
EPS = 1e-5

PAIRS = TOKENS // (2 * P)
SC = 512
STEPS = 2 * SLOTS // SC
PIECE = 1024
PIECES = SLOTS // PIECE
T_LAG = 6
PV_LAG = 9

BT = 512
BLOCKS = TOKENS // BT
HC = HID // P

W_AT, W_COLS = {}, 0
for _name, _cols in (("w1", HID), ("w2", HID), ("h1", HC * HID), ("h2", HC * HID), ("w3", HC * P)):
    W_AT[_name] = W_COLS
    W_COLS += _cols


def is_step(index, step):
    return isinstance(index, int) and index == step


def at_least(eng, sem, value):
    if isinstance(value, int) and value <= 0:
        return
    eng.wait_ge(sem, value)


def valid(index, end):
    return not isinstance(index, int) or 0 <= index < end


def attention(nc, xT, wqT, bq, kT, v, weights, o_dram, o_stored, den, keys, w_raw, low_max):
    ctx = ExitStack()
    with ctx:
        def sb(name, shape, dt):
            return ctx.enter_context(nc.sbuf_tensor(name, shape, dt))

        def sem(name):
            return ctx.enter_context(nc.semaphore(name))

        k_hi, k_lo = keys[:, 0:SLOTS], keys[:, SLOTS:2 * SLOTS]
        v_hi = sb("v_hi", [P, SLOTS // P, P], FP32R)
        v_lo = sb("v_lo", [P, SLOTS // P, P], FP32R)
        s_buf = sb("s_buf", [P, 2, SLOTS], FP32)
        p16 = sb("p16", [P, 2, 2, 2, SLOTS], FP16)
        pT = sb("pT", [P, 4, 2, 4 * P], FP32R)
        q_buf = sb("q_buf", [P, 2, 2, 2 * P], FP32R)
        x_in = sb("x_in", [P, 2 * P], FP32)
        o_tmp = sb("o_tmp", [P, 2 * P], FP32)
        o_sum = sb("o_sum", [P, 2 * P], FP32)
        ident = sb("ident", [P, P], FP16)
        wq = sb("wq", [P, P], FP32)
        bq_col = sb("bq_col", [P, 1], FP32)
        part_max = sb("part_max", [P, 2, PIECES], FP32)
        row_max = sb("row_max", [P, 2], FP32)
        bias = sb("bias", [P, 2], FP32)
        low_parts = sb("low_parts", [P, 4], FP32)
        table_spare = sb("exp_table_spare", [P, 1], FP32)
        k_raw = p16[:, 0, 1, :, :].rearrange("p a n -> p (a n)").bitcast(FP32)
        v_raw = p16[:, 1, 1, :, :].rearrange("p a n -> p (a n)").bitcast(FP32)

        s_ps = ctx.enter_context(nc.psum_tensor("s_ps", [P, 2, PIECE], FP32))
        t_ps = ctx.enter_context(nc.psum_tensor("t_ps", [P, 2, 2, 4 * P], FP16))
        o_ps = ctx.enter_context(nc.psum_tensor("o_ps", [P, 2, 4 * P], FP32))

        k_loaded = [sem(f"k_loaded{n}") for n in range(PIECES)]
        v_loaded = [sem(f"v_loaded{n}") for n in range(PIECES)]
        wq_loaded, bq_loaded, w_loaded = map(sem, ("wq_loaded", "bq_loaded", "w_loaded"))
        x_loaded, q_projected, q_high, q_split = map(sem, ("x_loaded", "q_projected", "q_high", "q_split"))
        ident_ready, k_high, v_high, v_split = map(sem, ("ident_ready", "k_high", "v_high", "v_split"))
        k_split = [sem(f"k_split{n}") for n in range(PIECES)]
        scored, bias_ready, exped, highed, split = map(sem, ("scored", "bias_ready", "exped", "highed", "split"))
        scores_moved, row_maxed = sem("scores_moved"), sem("row_maxed")
        transposed, pT_ready, pv_done = map(sem, ("transposed", "pT_ready", "pv_done"))
        o_half, o_ready = sem("o_half"), sem("o_ready")
        spare_ready = sem("spare_ready")
        w_high, w_low, w_maxed, low_found = map(sem, ("w_high", "w_low", "w_maxed", "low_found"))

        v_hi_flat = v_hi[:, :, :].rearrange("p c d -> p (c d)")
        v_lo_flat = v_lo[:, :, :].rearrange("p c d -> p (c d)")

        def piece(t, n):
            return t[:, n * PIECE:(n + 1) * PIECE]

        def split_piece(f, par, j):
            if j == 0:
                return f - 1, 0, PIECES - 1, 1 - par
            if j <= PIECES:
                return f - 1, 1, j - 1, 1 - par
            return f, 0, j - PIECES - 1, par

        def by_act(f, j):
            return is_step(f, 0) and j > PIECES or is_step(f, 1) and j < T_LAG // 2 + 1

        def p_high(p, tile, k, par, eng, round_to):
            eng.wait_ge(exped, 8 * p + 4 * tile + k + 1)
            if tile == 0 and k == 0:
                at_least(eng, transposed, 16 * p - 16)
            if is_step(p, 1) and tile == 1 and k == 0:
                eng.wait_ge(v_split, PIECES)
            round_to(piece(p16[:, par, tile, 0, :], k), piece(s_buf[:, tile, :], k)).then_inc(highed, 1)

        def k_low_part(eng, ops, n):
            eng.wait_ge(k_high, n + 1)
            ops.tensor_tensor(piece(k_lo, n), piece(k_raw, n), piece(k_hi, n).bitcast(FP32), ALU.subtract).then_inc(k_split[n], 1)

        def frames(eng, frame):
            frame(0, 0)
            frame(1, 1)
            with eng.Fori(1, PAIRS // 2 - 1) as half:
                frame(half * 2, 0)
                frame(half * 2 + 1, 1)
            for f in range(PAIRS - 2, PAIRS + 2):
                frame(f, f % 2)

        def unit_bank(par, j):
            return (par + j + (j >= PIECES)) % 2

        block_ctx = ctx.enter_context(nc.Block())

        @block_ctx.sync
        def _(sp):
            def load_x(pair):
                sp.dma_start(x_in[:, :], xT[:, bass.ds(pair * 2 * P, 2 * P)]).then_inc(x_loaded, 16)

            load_x(0)
            sp.dma_start(wq[:, :], wqT).then_inc(wq_loaded, 16)
            sp.dma_start(bq_col[:, :], bq).then_inc(bq_loaded, 16)
            for n in range(PIECES):
                sp.dma_start(piece(k_raw, n), piece(kT, n)).then_inc(k_loaded[n], 16)
            sp.wait_ge(q_projected, 1)
            load_x(1)
            for n in range(PIECES):
                rows = PIECE // P
                sp.dma_start(piece(v_raw, n).rearrange("p (c d) -> p c d", d=P),
                             v[:, n * rows:(n + 1) * rows, :]).then_inc(v_loaded[n], 16)
            for name, t in weights.items():
                rows = t.shape[0] // P
                cols = rows * t.shape[1]
                sp.dma_start(w_raw[:, W_AT[name]:W_AT[name] + cols].rearrange("p (k n) -> p k n", k=rows),
                             t.rearrange("(k p) n -> p k n", p=P)).then_inc(w_loaded, 16)

            def frame(f, par):
                if valid(f + 2, PAIRS):
                    sp.wait_ge(q_projected, f + 2)
                    load_x(f + 2)
                if valid(f - 2, PAIRS):
                    sp.wait_ge(o_ready, f - 1)
                    sp.dma_start(o_dram[:, bass.ds((f - 2) * 2 * P, 2 * P)], o_sum[:, :]).then_inc(o_stored, 16)

            frames(sp, frame)

        @block_ctx.gpsimd
        def _(pool):
            nc.gpsimd.memset(table_spare[:, :], 0.0).then_inc(spare_ready, 1)
            nc.gpsimd.memset(ident[:, :], 0.0).then_inc(ident_ready, 1)
            pool.wait_ge(ident_ready, 1)
            nc.gpsimd.affine_select(out=ident[:, :], in_=ident[:, :], compare_op=ALU.not_equal, fill=1.0, base=0,
                                    pattern=[[-1, P]], channel_multiplier=1).then_inc(ident_ready, 1)
            for n in range(1, PIECES, 2):
                k_low_part(pool, nc.gpsimd, n)
            for n in range(PIECES):
                pool.wait_ge(v_high, n + 1)
                nc.gpsimd.tensor_tensor(piece(v_lo_flat, n), piece(v_raw, n), piece(v_hi_flat, n).bitcast(FP32),
                                        ALU.subtract).then_inc(v_split, 1)
            pool.wait_ge(w_maxed, 4)
            nc.gpsimd.partition_all_reduce(low_max[:, :], low_parts[:, 3:4], P, bass.bass_isa.ReduceOp.max).then_inc(low_found, 1)
            pool.wait_ge(low_found, 1)

        @block_ctx.scalar
        def _(act):
            def q_high_part(p, par):
                act.wait_ge(q_projected, p + 1)
                at_least(act, scored, 8 * p - 8)
                nc.scalar.activation(q_buf[:, par, 0, :], s_ps[:, 1 - par, 0:2 * P], ACT.Identity,
                                     bias=bq_col[:, :]).then_inc(q_high, 1)

            act.wait_ge(spare_ready, 1)
            nc.scalar.activation(table_spare[:, :], table_spare[:, :], ACT.Exp).then_inc(spare_ready, 1)
            act.wait_ge(bq_loaded, 16)
            q_high_part(0, 0)
            for n in range(PIECES):
                act.wait_ge(k_loaded[n], 16)
                nc.scalar.activation(piece(k_hi, n), piece(k_raw, n), ACT.Copy).then_inc(k_high, 1)

            def exp_piece(p, tile, k):
                act.wait_ge(bias_ready, 2 * p + tile + 1)
                s = piece(s_buf[:, tile, :], k)
                nc.scalar.activation(s, s, ACT.Exp, bias=bias[:, tile:tile + 1], scale=SCALE,
                                     accum_out=den[:, bass.ds((2 * p + tile) * PIECES + k, 1)]).then_inc(exped, 1)

            def act_copy(out, src):
                return nc.scalar.activation(out, src, ACT.Copy)

            def frame(f, par):
                for t in range(STEPS):
                    u = 16 * f + (t - 16 - T_LAG)
                    if valid(u, 16 * PAIRS):
                        act.wait_ge(transposed, u + 1)
                        at_least(act, pv_done, u - 3)
                        nc.scalar.activation(pT[:, t % 4, :, :], t_ps[:, t % 2, :, :], ACT.Copy).then_inc(pT_ready, 1)
                    if t == 8 and valid(f + 1, PAIRS):
                        q_high_part(f + 1, 1 - par)
                    if t % 2 == 0:
                        tile, k = (1, t // 2) if t < 8 else (0, (t - 8) // 2)
                        if valid(f - tile, PAIRS):
                            exp_piece(f - tile, tile, k)
                        if by_act(f, t // 2):
                            p_high(*split_piece(f, par, t // 2), act, act_copy)
                    if is_step(f, 0) and t in (4, 5, 6, 7):
                        n = t - 4
                        act.wait_ge(v_loaded[n], 16)
                        nc.scalar.activation(piece(v_hi_flat, n), piece(v_raw, n), ACT.Copy).then_inc(v_high, 1)
                    if t == 11 and valid(f - 2, PAIRS):
                        act.wait_ge(pv_done, 16 * f - 16)
                        at_least(act, o_ready, f - 2)
                        nc.scalar.activation(o_tmp[:, :], o_ps[:, par, 2 * P:], ACT.Copy).then_inc(o_half, 1)

            frames(act, frame)

        @block_ctx.vector
        def _(dve):
            def q_low_part(p, par):
                dve.wait_ge(q_high, p + 1)
                nc.vector.scalar_tensor_tensor(out=q_buf[:, par, 1, :], in0=s_ps[:, 1 - par, 0:2 * P],
                                               scalar=bq_col[:, :], in1=q_buf[:, par, 0, :].bitcast(FP32),
                                               op0=ALU.add, op1=ALU.subtract).then_inc(q_split, 1)

            q_low_part(0, 0)
            for n in range(0, PIECES, 2):
                k_low_part(dve, nc.vector, n)

            def p_low(p, tile, k, par):
                dve.wait_ge(highed, 8 * p + 4 * tile + k + 1)
                nc.vector.tensor_tensor(piece(p16[:, par, tile, 1, :], k), piece(s_buf[:, tile, :], k),
                                        piece(p16[:, par, tile, 0, :], k), ALU.subtract).then_inc(split, 1)

            def find_low_weights():
                dve.wait_ge(w_loaded, 16 * len(weights))
                dve.wait_ge(scored, 8 * PAIRS)
                nc.vector.tensor_copy(keys[:, 0:W_COLS], w_raw[:, :]).then_inc(w_high, 1)
                dve.wait_ge(w_high, 1)
                room = 2 * SLOTS - W_COLS
                for n, at in enumerate(range(0, W_COLS, room)):
                    cols = min(room, W_COLS - at)
                    left = keys[:, W_COLS:W_COLS + cols]
                    at_least(dve, w_maxed, n)
                    nc.vector.tensor_tensor(left, w_raw[:, at:at + cols], keys[:, at:at + cols].bitcast(FP32),
                                            ALU.subtract).then_inc(w_low, 1)
                    dve.wait_ge(w_low, n + 1)
                    nc.vector.reduce_max(low_parts[:, n:n + 1], left.bitcast(FP32), AX.X, apply_absolute_value=True).then_inc(w_maxed, 1)
                dve.wait_ge(w_maxed, 3)
                nc.vector.reduce_max(low_parts[:, 3:4], low_parts[:, 0:3], AX.X).then_inc(w_maxed, 1)

            def frame(f, par):
                for j in range(2 * PIECES):
                    tile, k = divmod(j, PIECES)
                    before = split_piece(f, par, j)
                    if j == PIECES and valid(f + 1, PAIRS):
                        q_low_part(f + 1, 1 - par)
                    if valid(f, PAIRS):
                        dve.wait_ge(scored, 8 * f + j + 1)
                        at_least(dve, split, 8 * f - 8 + 4 * tile + k + 1)
                        nc.vector.tensor_scalar(piece(s_buf[:, tile, :], k), s_ps[:, unit_bank(par, j), :], 1.0, None,
                                                ALU.mult, ALU.max, accum_out=part_max[:, tile, k:k + 1]).then_inc(scores_moved, 1)
                    if valid(before[0], PAIRS) and not by_act(f, j):
                        p_high(*before, dve, nc.vector.tensor_copy)
                    if valid(f, PAIRS) and k == PIECES - 1:
                        dve.wait_ge(scores_moved, 8 * f + j + 1)
                        nc.vector.reduce_max(row_max[:, tile:tile + 1], part_max[:, tile, :], AX.X).then_inc(row_maxed, 1)
                        dve.wait_ge(row_maxed, 2 * f + tile + 1)
                        nc.vector.tensor_scalar(bias[:, tile:tile + 1], row_max[:, tile:tile + 1], -SCALE, LIFT,
                                                ALU.mult, ALU.add).then_inc(bias_ready, 1)
                    if valid(before[0], PAIRS):
                        p_low(*before)
                    if is_step(f, PAIRS) and j == 5:
                        find_low_weights()
                    if j == 7 and valid(f - 2, PAIRS):
                        dve.wait_ge(o_half, f - 1)
                        at_least(dve, o_stored, 16 * (f - 2))
                        nc.vector.tensor_tensor(o_sum[:, :], o_ps[:, par, 0:2 * P], o_tmp[:, :], ALU.add).then_inc(o_ready, 1)

            frames(dve, frame)

        @block_ctx.tensor
        def _(pe):
            def q_project(p, bank):
                pe.wait_ge(x_loaded, 16 * (p + 1))
                nc.tensor.matmul(s_ps[:, bank, 0:2 * P], wq[:, :], x_in[:, :], start=True, stop=True).then_inc(q_projected, 1)

            pe.wait_ge(wq_loaded, 16)
            q_project(0, 1)

            def frame(f, par):
                if is_step(f, 0):
                    pe.wait_ge(q_split, 1)
                if is_step(f, 1):
                    pe.wait_ge(ident_ready, 2)
                for t in range(STEPS):
                    for ahead in (0, 1) if t % 2 == 0 else ():
                        u = 16 * f + (t + ahead - 16 - T_LAG)
                        if valid(u, 16 * PAIRS):
                            p, pp, s = (f - 1, 1 - par, t + ahead - T_LAG) if t >= T_LAG else (f - 2, par, t + ahead + 16 - T_LAG)
                            if s % 4 == 0:
                                pe.wait_ge(split, 8 * p + 4 + s // 4 + 1)
                            at_least(pe, pT_ready, u - 1)
                            for c in range(2):
                                for part in range(2):
                                    for tile in range(2):
                                        at = (2 * s + c) * P
                                        last = nc.tensor.transpose(
                                            t_ps[:, ahead, c, (2 * part + tile) * P:(2 * part + tile + 1) * P],
                                            p16[:, pp, tile, part, at:at + P], ident[:, :])
                            last.then_inc(transposed, 1)
                    if valid(f, PAIRS):
                        tile, c = divmod(t, STEPS // 2)
                        j = t // 2
                        if t == STEPS // 2 and valid(f + 1, PAIRS):
                            at_least(pe, scores_moved, 8 * f + 3)
                            q_project(f + 1, par)
                        if t % 2 == 0:
                            if j == PIECES + 1 and valid(f + 1, PAIRS):
                                pe.wait_ge(q_split, f + 2)
                            elif j == PIECES + 1:
                                pe.wait_ge(scores_moved, 8 * f + 4)
                            else:
                                at_least(pe, scores_moved, 8 * f + j - 1 + (j == PIECES))
                            if is_step(f, 0) and tile == 0:
                                pe.wait_ge(k_split[j], 1)
                        out = s_ps[:, unit_bank(par, j), (t % 2) * SC:(t % 2 + 1) * SC]
                        q_h = q_buf[:, par, 0, tile * P:(tile + 1) * P]
                        q_l = q_buf[:, par, 1, tile * P:(tile + 1) * P]
                        k_h, k_l = k_hi[:, c * SC:(c + 1) * SC], k_lo[:, c * SC:(c + 1) * SC]
                        nc.tensor.matmul(out, q_h, k_h, start=True, stop=False)
                        nc.tensor.matmul(out, q_h, k_l, start=False, stop=False)
                        last = nc.tensor.matmul(out, q_l, k_h, start=False, stop=True)
                        if t % 2 == 1:
                            last.then_inc(scored, 1)
                    w = 16 * f + (t - 16 - PV_LAG)
                    if valid(w, 16 * PAIRS):
                        p, pp, s = (f - 1, 1 - par, t - PV_LAG) if t >= PV_LAG else (f - 2, par, t + 16 - PV_LAG)
                        pe.wait_ge(pT_ready, w + 1)
                        if s == 0:
                            at_least(pe, o_ready, p - 1)
                            if is_step(f, 1):
                                pe.wait_ge(v_split, PIECES)
                        for c in range(2):
                            first, final = s == 0 and c == 0, s == STEPS - 1 and c == 1
                            nc.tensor.matmul(o_ps[:, pp, :], v_hi[:, 2 * s + c, :], pT[:, (t - PV_LAG + T_LAG) % 4, c, :],
                                             start=first, stop=False, skip_group_check=True)
                            last = nc.tensor.matmul(o_ps[:, pp, 0:2 * P], v_lo[:, 2 * s + c, :],
                                                    pT[:, (t - PV_LAG + T_LAG) % 4, c, 0:2 * P],
                                                    start=False, stop=final, skip_group_check=True)
                        last.then_inc(pv_done, 1)

            frames(pe, frame)


def ffn(nc, x_rows, woT, bo, scale_cols, o_dram, o_stored, den, keys, w_raw, low_max, out_rows):
    ctx = ExitStack()
    with ctx:
        def sb(name, shape, dt):
            return ctx.enter_context(nc.sbuf_tensor(name, shape, dt))

        def sem(name):
            return ctx.enter_context(nc.semaphore(name))

        w_hi = keys[:, 0:W_COLS]
        w_lo = sb("w_lo", [P, W_COLS], FP32R)
        wo_raw = sb("wo_raw", [P, P], FP32)
        wo_hi = sb("wo_hi", [P, P], FP32R)
        wo_lo = sb("wo_lo", [P, P], FP32R)
        scales = sb("scales", [P, 4 * HC + 1], FP32)
        bo_all = sb("bo_all", [P, P], FP32)
        den_sum = sb("den_sum", [P, TOKENS // P], FP32)
        rden = sb("rden", [P, TOKENS // P], FP32)
        ident = sb("ident2", [P, P], FP32)
        minus_half = sb("minus_half", [P, 4], FP32)
        eps = sb("eps", [P, 4], FP32)
        spare = sb("spare", [P, 2], FP32)
        o_in = sb("o_in", [P, 2, BT], FP32)
        x_in = sb("x_in2", [P, 2, 4, P], FP32)
        xb = sb("xb", [P, 4, P], FP32)
        o_hi = sb("o_hi", [P, BT], FP32R)
        o_lo = sb("o_lo", [P, BT], FP32R)
        z1 = sb("z1", [P, 4, P], FP32)
        x1 = sb("x1", [P, 4, P], FP32)
        stats = sb("stats", [P, 2, 4, 6], FP32)
        moments = sb("moments", [P, 2, 4, 2], FP32)
        rstd = sb("rstd", [P, 2, 4], FP32)
        var_eps = sb("var_eps", [P, 2, 4], FP32)
        x1T = sb("x1T", [P, TOKENS], FP32)
        x1_hi = sb("x1_hi", [P, BT], FP32R)
        x1_lo = sb("x1_lo", [P, BT], FP32R)
        table_spare = sb("table_spare", [P, 2], FP32)
        gelu = sb("gelu", [P, 2, HC, BT], FP32)
        chunk_size = HC * BT
        gate = w_raw[:, 0:chunk_size].rearrange("p (j n) -> p j n", j=HC)
        prod = w_raw[:, chunk_size:2 * chunk_size].rearrange("p (j n) -> p j n", j=HC)
        h_hi = sb("h_hi", [P, 3, HC, BT], FP32R)
        h_lo = sb("h_lo", [P, 3, HC, BT], FP32R)
        z2T = sb("z2T", [P, BT], FP32)
        y_out = sb("y_out", [P, 2, 4, P], FP32)

        ring = ctx.enter_context(nc.psum_tensor("ring", [P, 4, BT], FP32))
        y3_ps = ctx.enter_context(nc.psum_tensor("y3_ps", [P, BT], FP32))
        y_ps = ctx.enter_context(nc.psum_tensor("y_ps", [P, 4, P], FP32))
        x1_ps = ctx.enter_context(nc.psum_tensor("x1_ps", [P, BT], FP32))
        z2_ps = ctx.enter_context(nc.psum_tensor("z2_ps", [P, 4, P], FP32))

        wo_loaded, bo_loaded, scales_loaded = sem("wo_loaded"), sem("bo_loaded"), sem("scales_loaded")
        wo_high, wo_split, w_split, rden_ready, const_ready = map(
            sem, ("wo_high", "wo_split", "w_split", "rden_ready", "const_ready"))
        o_loaded = [sem("oo_loaded0"), sem("oo_loaded1")]
        x_loaded = [sem("xx_loaded0"), sem("xx_loaded1")]
        o_high, o_split, xb_ready, y_done = map(sem, ("o_high", "o_split", "xb_ready", "y_done"))
        z1_ready, stats1_ready, moments1_ready, var1_ready, rstd1_ready, x1_ready = map(
            sem, ("z1_ready", "stats1_ready", "moments1_ready", "var1_ready", "rstd1_ready", "x1_ready"))
        x1_transposed, x1T_ready, x1_high, x1_split = map(sem, ("x1_transposed", "x1T_ready", "x1_high", "x1_split"))
        in_done, mid1_done, mid2_done = map(sem, ("in_done", "mid1_done", "mid2_done"))
        gated, prod_ready, prod_high, in_split = map(sem, ("gated", "prod_ready", "prod_high", "in_split"))
        gelu_f = [sem("gelu_f1"), sem("gelu_f2")]
        gelu_h = [sem("gelu_h1"), sem("gelu_h2")]
        gelu_split = [sem("gelu_split1"), sem("gelu_split2")]
        y3_done, z2T_ready, z2_transposed = map(sem, ("y3_done", "z2T_ready", "z2_transposed"))
        stats2_ready, moments2_ready, var2_ready, rstd2_ready, y_ready = map(
            sem, ("stats2_ready", "moments2_ready", "var2_ready", "rstd2_ready", "y_ready"))
        waited, table_loaded = sem("waited"), sem("table_loaded")
        y_stored = [sem("y_stored0"), sem("y_stored1")]

        def weight(t, name, k, j, width=HID):
            o = W_AT[name] + k * width + j * P
            return t[:, o:o + P]

        FIRST, LAST = -2, BLOCKS

        def filling(i):
            return isinstance(i, int) and i < 0

        def rows_blocks(i):
            if not filling(i):
                return (i + 2,) if valid(i + 2, BLOCKS) else ()
            return (0, 1) if i == FIRST else ()

        def turns(eng, turn):
            for i in range(FIRST, 2):
                turn(i, i // 2, i % 2)
            n = (BLOCKS - 6) // 2
            with eng.Fori(1, 1 + n) as half:
                turn(half * 2, half, 0)
                turn(half * 2 + 1, half, 1)
            for i in range(2 + 2 * n, LAST + 1):
                turn(i, i // 2, i % 2)

        block_ctx = ctx.enter_context(nc.Block())

        @block_ctx.sync
        def _(sp):
            def load(b, par):
                sp.dma_start(o_in[:, par, :], o_dram[:, bass.ds(b * BT, BT)]).then_inc(o_loaded[par], 16)
                sp.dma_start(x_in[:, par, :, :], x_rows[:, bass.ds(b * 4, 4), :]).then_inc(x_loaded[par], 16)

            sp.dma_start(wo_raw[:, :], woT).then_inc(wo_loaded, 16)
            load(0, 0)
            sp.dma_start(bo_all[:, :], bo.partition_broadcast(P)).then_inc(bo_loaded, 16)
            load(1, 1)
            for n, t in enumerate(scale_cols):
                sp.dma_start(scales[:, n * HC:n * HC + t.shape[1]], t).then_inc(scales_loaded, 16)
            sp.wait_ge(o_stored, 16 * PAIRS)

            def turn(i, i2, par):
                if valid(i - 1, BLOCKS):
                    sp.wait_ge(y_ready, 4 * i)
                    sp.dma_start(out_rows[:, bass.ds(4 * (i - 1), 4), :], y_out[:, 1 - par, :, :]).then_inc(y_stored[1 - par], 16)
                if valid(i + 2, BLOCKS) and valid(i + 4, BLOCKS):
                    sp.wait_ge(o_split, i + 3)
                    sp.wait_ge(xb_ready, i + 3)
                    load(i + 4, par)

            turns(sp, turn)
            for par in range(2):
                sp.wait_ge(y_stored[par], 16 * BLOCKS // 2)

        @block_ctx.gpsimd
        def _(pool):
            nc.gpsimd.memset(ident[:, :], 0.0).then_inc(const_ready, 1)
            nc.gpsimd.memset(minus_half[:, :], -0.5).then_inc(const_ready, 1)
            nc.gpsimd.memset(eps[:, :], EPS).then_inc(const_ready, 1)
            pool.wait_ge(const_ready, 3)
            nc.gpsimd.affine_select(out=ident[:, :], in_=ident[:, :], compare_op=ALU.not_equal, fill=1.0, base=0,
                                    pattern=[[-1, P]], channel_multiplier=1).then_inc(const_ready, 1)
            pool.wait_ge(bo_loaded, 16)

            def add_bias(b, b2, par):
                pool.wait_ge(x_loaded[par], 16 * b2 + 16)
                at_least(pool, z1_ready, 4 * b)
                nc.gpsimd.tensor_tensor(xb[:, :, :], x_in[:, par, :, :],
                                        bo_all[:, :].unsqueeze(1).broadcast_to([P, 4, P]), ALU.add).then_inc(xb_ready, 1)

            def inverse_deviation(b, which, moments_ready, var_ready, ready):
                pool.wait_ge(moments_ready, 4 * b + 4)
                nc.gpsimd.tensor_tensor(var_eps[:, which, :], moments[:, which, :, 1], eps[:, :], ALU.add).then_inc(var_ready, 1)
                pool.wait_ge(var_ready, b + 1)
                nc.gpsimd.tensor_tensor(rstd[:, which, :], var_eps[:, which, :], minus_half[:, :], ALU.pow).then_inc(ready, 1)

            def turn(i, i2, par):
                if valid(i + 2, BLOCKS):
                    add_bias(i + 2, i2 + 1, par)
                if valid(i + 2, BLOCKS):
                    inverse_deviation(i + 2, 0, moments1_ready, var1_ready, rstd1_ready)
                if valid(i - 1, BLOCKS):
                    inverse_deviation(i - 1, 1, moments2_ready, var2_ready, rstd2_ready)

            turns(pool, turn)

        @block_ctx.scalar
        def _(act):
            act.wait_ge(wo_loaded, 16)
            nc.scalar.activation(wo_hi[:, :], wo_raw[:, :], ACT.Copy).then_inc(wo_high, 1)

            act.wait_ge(const_ready, 4)

            def load_table(func):
                nc.scalar.activation(table_spare[:, 0:1], minus_half[:, 0:1], func).then_inc(table_loaded, 1)

            def o_high_part(b, b2, par):
                act.wait_ge(o_loaded[par], 16 * b2 + 16)
                at_least(act, y_done, b)
                nc.scalar.activation(o_hi[:, :], o_in[:, par, :], ACT.Copy).then_inc(o_high, 1)

            def gates(b):
                if is_step(b, 0):
                    act.wait_ge(scales_loaded, 16 * len(scale_cols))
                    act.wait_ge(w_split, 1)
                for j in (0, 1, 2, 3):
                    act.wait_ge(in_done, 8 * b + 2 * j + 1)
                    at_least(act, prod_ready, 4 * b + j - 3)
                    nc.scalar.activation(gate[:, j, :], ring[:, (2 * j) % 4, :], ACT.Silu,
                                         scale=scales[:, j:j + 1]).then_inc(gated, 1)
                    if j == HC - 1:
                        load_table(ACT.Gelu)
                    for k in (j - 1, j) if j % 2 else ():
                        act.wait_ge(prod_ready, 4 * b + k + 1)
                        if k == 0:
                            at_least(act, mid1_done, 4 * b)
                        nc.scalar.activation(h_hi[:, 0, k, :], prod[:, k, :], ACT.Copy).then_inc(prod_high, 1)

            def gelus(b, layer, done, used_by, chunks=range(HC)):
                col = (1 + layer) * HC
                for j in chunks:
                    act.wait_ge(done, 4 * b + j + 1)
                    at_least(act, gelu_split[layer - 1], 4 * b + j - 3)
                    nc.scalar.activation(gelu[:, layer - 1, j, :], ring[:, j, :], ACT.Gelu,
                                         scale=scales[:, col + j:col + j + 1]).then_inc(gelu_f[layer - 1], 1)
                    if j == 0:
                        at_least(act, *used_by)
                    nc.scalar.activation(h_hi[:, layer, j, :], ring[:, j, :], ACT.Gelu,
                                         scale=scales[:, col + j:col + j + 1]).then_inc(gelu_h[layer - 1], 1)

            def turn(i, i2, par):
                if valid(i + 1, BLOCKS):
                    load_table(ACT.Silu)
                if valid(i + 1, BLOCKS):
                    gates(i + 1)
                if valid(i + 3, BLOCKS):
                    o_high_part(i + 3, i2 + 1 + par, 1 - par)
                if valid(i, BLOCKS):
                    gelus(i, 2, mid2_done, (y3_done, i))
                if valid(i + 1, BLOCKS) and not filling(i):
                    gelus(i + 1, 1, mid1_done, (mid2_done, 4 * (i + 1)), (0,))
                if valid(i + 2, BLOCKS):
                    act.wait_ge(x1_transposed, i + 3)
                    nc.scalar.activation(x1T[:, bass.ds((i + 2) * BT, BT)], x1_ps[:, :], ACT.Copy).then_inc(x1T_ready, 1)
                if valid(i + 1, BLOCKS):
                    gelus(i + 1, 1, mid1_done, (mid2_done, 4 * (i + 1)), (0, 1, 2, 3) if filling(i) else (1, 2, 3))

            o_high_part(0, 0, 0)
            turns(act, turn)

        @block_ctx.vector
        def _(dve):
            nc.vector.reduce_sum(den_sum[:, :], den[:, :].rearrange("p (t k) -> p t k", k=PIECES), AX.X).then_inc(rden_ready, 1)
            dve.wait_ge(rden_ready, 1)
            nc.vector.reciprocal(rden[:, :], den_sum[:, :]).then_inc(rden_ready, 1)
            dve.wait_ge(wo_high, 1)
            nc.vector.tensor_tensor(wo_lo[:, :], wo_raw[:, :], wo_hi[:, :].bitcast(FP32), ALU.subtract).then_inc(wo_split, 1)
            low = dve.value_load(low_max[0:1, 0:1].bitcast(mybir.dt.int32))
            with dve.If(low > 0):
                nc.vector.tensor_tensor(w_lo[:, :], w_raw[:, :], w_hi.bitcast(FP32), ALU.subtract).then_inc(w_split, 1)
            with dve.Else():
                nc.vector.memset(spare[:, 0:1], 0.0).then_inc(w_split, 1)
            dve.wait_ge(rden_ready, 2)

            def o_low_part(b, par):
                dve.wait_ge(o_high, b + 1)
                nc.vector.tensor_tensor(o_lo[:, :], o_in[:, par, :], o_hi[:, :].bitcast(FP32), ALU.subtract).then_inc(o_split, 1)

            def products(b):
                if is_step(b, 0):
                    dve.wait_ge(scales_loaded, 16 * len(scale_cols))
                for step in range(HC + 1):
                    if step < HC:
                        j = step
                        dve.wait_ge(gated, 4 * b + j + 1)
                        dve.wait_ge(in_done, 8 * b + 2 * j + 2)
                        at_least(dve, prod_high, 4 * b + j - 3)
                        at_least(dve, in_split, 4 * b + j - 3)
                        nc.vector.scalar_tensor_tensor(out=prod[:, j, :], in0=ring[:, (2 * j + 1) % 4, :],
                                                       scalar=scales[:, HC + j:HC + j + 1], in1=gate[:, j, :],
                                                       op0=ALU.mult, op1=ALU.mult).then_inc(prod_ready, 1)
                    if step >= 1:
                        j = step - 1
                        dve.wait_ge(prod_high, 4 * b + j + 1)
                        nc.vector.tensor_tensor(h_lo[:, 0, j, :], prod[:, j, :],
                                                h_hi[:, 0, j, :].bitcast(FP32), ALU.subtract).then_inc(in_split, 1)

            def gelu_low(b, layer, j):
                dve.wait_ge(gelu_h[layer - 1], 4 * b + j + 1)
                nc.vector.tensor_tensor(h_lo[:, layer, j, :], gelu[:, layer - 1, j, :],
                                        h_hi[:, layer, j, :].bitcast(FP32), ALU.subtract).then_inc(gelu_split[layer - 1], 1)

            def moments_of(b, which, src, stats_ready, moments_ready):
                for s in range(4):
                    nc.vector.bn_stats(stats[:, which, s, :], src[:, s, :]).then_inc(stats_ready, 1)
                dve.wait_ge(stats_ready, 4 * b + 4)
                nc.vector.memset(spare[:, which:which + 1], 0.0).then_inc(waited, 1)
                for s in range(4):
                    nc.vector.bn_aggr(moments[:, which, s, :], stats[:, which, s, :]).then_inc(moments_ready, 1)

            def normalise(b, which, src, dst, rstd_ready, ready):
                dve.wait_ge(rstd_ready, b + 1)
                for s in range(4):
                    nc.vector.tensor_scalar(dst[:, s, :], src[:, s, :], moments[:, which, s, 0:1], rstd[:, which, s:s + 1],
                                            ALU.subtract, ALU.mult).then_inc(ready, 1)

            def residual(b):
                dve.wait_ge(y_done, b + 1)
                dve.wait_ge(xb_ready, b + 1)
                at_least(dve, x1_ready, 4 * b)
                for s in range(4):
                    nc.vector.scalar_tensor_tensor(out=z1[:, s, :], in0=y_ps[:, s, :],
                                                   scalar=rden[:, bass.ds(4 * b + s, 1)], in1=xb[:, s, :],
                                                   op0=ALU.mult, op1=ALU.add).then_inc(z1_ready, 1)
                dve.wait_ge(z1_ready, 4 * (b + 1))
                moments_of(b, 0, z1, stats1_ready, moments1_ready)

            def normalise_x1(b):
                at_least(dve, x1_transposed, b)
                normalise(b, 0, z1, x1, rstd1_ready, x1_ready)

            def turn(i, i2, par):
                if valid(i + 1, BLOCKS):
                    products(i + 1)
                for b in rows_blocks(i)[:1]:
                    residual(b)
                if valid(i + 3, BLOCKS):
                    o_low_part(i + 3, 1 - par)
                if valid(i - 1, BLOCKS):
                    dve.wait_ge(z2_transposed, i)
                    moments_of(i - 1, 1, z2_ps, stats2_ready, moments2_ready)
                for b in rows_blocks(i)[:1]:
                    normalise_x1(b)
                for b in rows_blocks(i)[1:]:
                    residual(b)
                if valid(i - 1, BLOCKS):
                    at_least(dve, y_stored[1 - par], 16 * (i2 - 1 + par))
                    normalise(i - 1, 1, z2_ps, y_out[:, 1 - par, :, :], rstd2_ready, y_ready)
                if valid(i, BLOCKS):
                    for j in range(HC):
                        gelu_low(i, 2, j)
                if valid(i + 1, BLOCKS):
                    gelu_low(i + 1, 1, 0)
                    gelu_low(i + 1, 1, 1)
                if valid(i + 2, BLOCKS):
                    dve.wait_ge(x1T_ready, i + 3)
                    at_least(dve, in_done, 8 * (i + 2))
                    src = x1T[:, bass.ds((i + 2) * BT, BT)]
                    nc.vector.tensor_copy(x1_hi[:, :], src).then_inc(x1_high, 1)
                    dve.wait_ge(x1_high, i + 3)
                    nc.vector.tensor_tensor(x1_lo[:, :], src, x1_hi[:, :].bitcast(FP32), ALU.subtract).then_inc(x1_split, 1)
                for b in rows_blocks(i)[1:]:
                    normalise_x1(b)
                if valid(i + 1, BLOCKS):
                    gelu_low(i + 1, 1, 2)
                    gelu_low(i + 1, 1, 3)
                if valid(i, BLOCKS):
                    dve.wait_ge(y3_done, i + 1)
                    at_least(dve, z2_transposed, i)
                    nc.vector.scalar_tensor_tensor(out=z2T[:, :], in0=y3_ps[:, :], scalar=scales[:, 4 * HC:4 * HC + 1],
                                                   in1=x1T[:, bass.ds(i * BT, BT)], op0=ALU.mult, op1=ALU.add).then_inc(z2T_ready, 1)

            o_low_part(0, 0)
            turns(dve, turn)

        @block_ctx.tensor
        def _(pe):
            pe.wait_ge(w_split, 1)
            pe.wait_ge(wo_split, 1)
            pe.wait_ge(const_ready, 4)

            def split_products(out, pairs, sem_done, low_weights, parts_ready=None):
                for n, (wh, wl, hh, hl) in enumerate(pairs):
                    if parts_ready:
                        pe.wait_ge(parts_ready[0], parts_ready[1] + n + 1)
                    final = n == len(pairs) - 1
                    nc.tensor.matmul(out, wh, hh, start=n == 0, stop=False)
                    last = nc.tensor.matmul(out, wh, hl, start=False, stop=final and not low_weights)
                    if low_weights:
                        last = nc.tensor.matmul(out, wl, hh, start=False, stop=final)
                last.then_inc(sem_done, 1)

            def layer(out, name, j, src, sem_done, low_weights, width=HID, parts_ready=None):
                split_products(out, [(weight(w_hi, name, k, j, width), weight(w_lo, name, k, j, width),
                                      h_hi[:, src, k, :], h_lo[:, src, k, :]) for k in range(HC)], sem_done, low_weights,
                               parts_ready if j == 0 else None)

            def bank_read_by_in(b, bank):
                pe.wait_ge((gated, prod_ready)[bank % 2], 4 * b + 3 + bank // 2)

            def turn(i, i2, par, low_weights):
                def first_layer(chunks):
                    b = i + 1
                    for j in chunks:
                        for n, name in enumerate(("w1", "w2")):
                            bank = (2 * j + n) % 4
                            if j < 2:
                                at_least(pe, gelu_h[0], 4 * i + bank + 1)
                            elif n == 0:
                                pe.wait_ge(gated, 4 * b + j - 1)
                            else:
                                pe.wait_ge(prod_ready, 4 * b + j - 1)
                            split_products(ring[:, bank, :], [(weight(w_hi, name, 0, j), weight(w_lo, name, 0, j),
                                                               x1_hi[:, :], x1_lo[:, :])], in_done, low_weights)
                if valid(i + 1, BLOCKS):
                    pe.wait_ge(x1_split, i + 2)
                    first_layer((0, 1))
                for b in rows_blocks(i):
                    pe.wait_ge(o_split, b + 1)
                    at_least(pe, z1_ready, 4 * b)
                    wh, wl = wo_hi[:, :], wo_lo[:, :]
                    for s in range(4):
                        oh, ol = o_hi[:, s * P:(s + 1) * P], o_lo[:, s * P:(s + 1) * P]
                        nc.tensor.matmul(y_ps[:, s, :], oh, wh, start=True, stop=False)
                        nc.tensor.matmul(y_ps[:, s, :], oh, wl, start=False, stop=False)
                        last = nc.tensor.matmul(y_ps[:, s, :], ol, wh, start=False, stop=True)
                    last.then_inc(y_done, 1)
                if valid(i + 1, BLOCKS):
                    first_layer((2, 3))
                if valid(i - 1, BLOCKS):
                    pe.wait_ge(z2T_ready, i)
                    at_least(pe, y_ready, 4 * (i - 1))
                    for s in range(4):
                        last = nc.tensor.transpose(z2_ps[:, s, :], z2T[:, s * P:(s + 1) * P], ident[:, :])
                    last.then_inc(z2_transposed, 1)
                if valid(i, BLOCKS):
                    for j in range(HC):
                        if valid(i + 1, BLOCKS):
                            bank_read_by_in(i + 1, j)
                        else:
                            pe.wait_ge(gelu_h[0], 4 * i + j + 1)
                        layer(ring[:, j, :], "h2", j, 1, mid2_done, low_weights, parts_ready=(gelu_split[0], 4 * i))
                def norm_transpose():
                    pe.wait_ge(x1_ready, 4 * (i + 3))
                    at_least(pe, x1T_ready, i + 2)
                    for s in range(4):
                        last = nc.tensor.transpose(x1_ps[:, s * P:(s + 1) * P], x1[:, s, :], ident[:, :])
                    last.then_inc(x1_transposed, 1)

                if filling(i):
                    norm_transpose()
                for j in range(HC):
                    if valid(i + 1, BLOCKS):
                        if valid(i, BLOCKS):
                            pe.wait_ge(gelu_h[1], 4 * i + j + 1)
                        else:
                            bank_read_by_in(i + 1, j)
                        layer(ring[:, j, :], "h1", j, 0, mid1_done, low_weights, parts_ready=(in_split, 4 * (i + 1)))
                    if j == 0 and valid(i + 2, BLOCKS) and not filling(i):
                        norm_transpose()
                if valid(i, BLOCKS):
                    at_least(pe, z2T_ready, i)
                    layer(y3_ps[:, :], "w3", 0, 2, y3_done, low_weights, P, (gelu_split[1], 4 * i))

            low = pe.value_load(low_max[0:1, 0:1].bitcast(mybir.dt.int32))
            with pe.If(low > 0):
                turns(pe, lambda i, i2, par: turn(i, i2, par, True))
            with pe.Else():
                turns(pe, lambda i, i2, par: turn(i, i2, par, False))


def program(nc, t, out):
    o_dram = nc.dram_tensor("o_scratch", (P, TOKENS), FP32).ap()
    with (
        nc.sbuf_tensor("den", [P, PIECES * TOKENS // P], FP32) as den,
        nc.sbuf_tensor("keys", [P, 2 * SLOTS], FP32R) as keys,
        nc.sbuf_tensor("w_raw", [P, W_COLS], FP32) as w_raw,
        nc.sbuf_tensor("low_max", [P, 1], FP32) as low_max,
        nc.semaphore("o_stored") as o_stored,
    ):
        weights = {"w1": t["w1T"], "w2": t["w2T"], "h1": t["h1T"], "h2": t["h2T"], "w3": t["w3T"]}
        attention(nc, t["xT"], t["wqT"], t["bq"], t["kT"], t["v"].rearrange("(c p) d -> p c d", p=P), weights,
                  o_dram, o_stored, den, keys, w_raw, low_max)
        rows = "(t p) d -> p t d"
        ffn(nc, t["x"].rearrange(rows, p=P), t["woT"], t["bo"], (t["s1"], t["s2"], t["s_h1"], t["s_h2"], t["s3"]),
            o_dram, o_stored, den, keys, w_raw, low_max, out.rearrange(rows, p=P))


def kernel(**inputs):
    import concourse.bacc as bacc
    from concourse.bass_utils import run_bass_kernel_spmd

    a = {n: np.asarray(v) for n, v in inputs.items()}
    x = a["L0_attn_hidden_states"].reshape(TOKENS, P)
    lay = np.ascontiguousarray
    arrays = {
        "x": lay(x), "xT": lay(x.T), "wqT": lay(a["L0_attn_Wq"].T), "woT": lay(a["L0_attn_Wo"].T),
        "bq": lay(a["L0_attn_bq"].reshape(P, 1)), "bo": lay(a["L0_attn_bo"]),
        "kT": lay(a["L0_attn_memory_keys"][0].T), "v": lay(a["L0_attn_memory_values"][0]),
        "w1T": lay(a["L0_ffn_w1_w"].T), "w2T": lay(a["L0_ffn_w2_w"].T), "h1T": lay(a["L0_ffn_h1_w"].T),
        "h2T": lay(a["L0_ffn_h2_w"].T), "w3T": lay(a["L0_ffn_w3_w"].T),
        "s1": lay(a["L0_ffn_w1_s"].reshape(HC, P).T), "s2": lay(a["L0_ffn_w2_s"].reshape(HC, P).T),
        "s_h1": lay(a["L0_ffn_h1_s"].reshape(HC, P).T), "s_h2": lay(a["L0_ffn_h2_s"].reshape(HC, P).T),
        "s3": lay(a["L0_ffn_w3_s"].reshape(P, 1)),
    }
    nc = bacc.Bacc("TRN2", target_bir_lowering=False, num_devices=1)
    t = {n: nc.dram_tensor(f"in_{n}", v.shape, mybir.dt.from_np(v.dtype), kind="ExternalInput").ap()
         for n, v in arrays.items()}
    out = nc.dram_tensor("out_0", (TOKENS, P), FP32, kind="ExternalOutput").ap()
    program(nc, t, out)
    r = run_bass_kernel_spmd(nc, [{f"in_{n}": v for n, v in arrays.items()}], core_ids=[0])
    return r.results[0]["out_0"].reshape(32, 256, P)
```
